# Optimizing a Trainium2 kernel written in Bass

```python
import numpy as np
import jax
import jax.numpy as jnp

def _softmax(x, axis=-1):
    return jax.nn.softmax(x, axis=axis)

def _gelu(x):
    return jax.nn.gelu(x, approximate=True)

def _silu(x):
    return jax.nn.silu(x)

def _sigmoid(x):
    return jax.nn.sigmoid(x)

def _layernorm(x, axis=-1, eps=1e-05):
    m = jnp.mean(x, axis=axis, keepdims=True)
    v = jnp.var(x, axis=axis, keepdims=True)
    return (x - m) / jnp.sqrt(v + eps)

def _scatter_add(tgt, idx, src, axis=0):
    return tgt.at[idx].add(src)

def _segment_sum(src, seg, n):
    return jax.ops.segment_sum(src, seg, n)
kernel_name = 'mk_sandwich_d1_jaxref_r4_282a9a'

def setup_inputs(seed: int=0):
    np.random.seed(seed)
    _w = jnp.asarray

    def _L0_attn_setup():
        import jax, jax.numpy as jnp
        import numpy as np
        from jax import lax
        B, L, H = (2, 256, 512)
        E, N, TR, K = (1024, 16, 128, 4)
        key = jax.random.key(seed)
        ks = jax.random.split(key, 10)
        s = lambda d: 1.0 / np.sqrt(d)
        return {'input_states': jax.random.normal(ks[0], (B, L, H), jnp.float32), 'W_in': jax.random.normal(ks[1], (H, 2 * E), jnp.float32) * s(H), 'conv_kernel': jax.random.normal(ks[2], (E, 1, K), jnp.float32) * s(K), 'conv_bias': jax.random.normal(ks[3], (E,), jnp.float32) * 0.01, 'W_x': jax.random.normal(ks[4], (E, TR + 2 * N), jnp.float32) * s(E), 'W_dt': jax.random.normal(ks[5], (TR, E), jnp.float32) * s(TR), 'b_dt': jax.random.normal(ks[6], (E,), jnp.float32) * 0.01, 'W_out': jax.random.normal(ks[7], (E, H), jnp.float32) * s(E), 'A_log': jax.random.uniform(ks[8], (E, N), jnp.float32, 0.0, 2.0), 'D': jax.random.normal(ks[9], (E,), jnp.float32)}
    _L0_attn_in = _L0_attn_setup()

    def _L0_ffn_setup():
        import jax, jax.numpy as jnp
        import numpy as np
        E = 32
        G = 8
        TKG = 4
        K = 4
        D = 512
        H = 256
        HS = 1024
        SCALE = 2.5
        CAP = 256

        def relu2(x):
            r = jnp.maximum(x, 0.0)
            return r * r

        def route_tokens(scores, bias_corr):
            T = scores.shape[0]
            scores_c = scores + bias_corr
            group_scores = jax.lax.top_k(scores_c.reshape(T, G, E // G), 2)[0].sum(-1)
            _, group_idx = jax.lax.top_k(group_scores, TKG)
            group_mask = jnp.zeros((T, G), scores.dtype).at[jnp.arange(T)[:, None], group_idx].set(1.0)
            score_mask = jnp.repeat(group_mask, E // G, axis=1)
            masked = jnp.where(score_mask > 0, scores_c, 0.0)
            _, topk_idx = jax.lax.top_k(masked, K)
            topk_w = jnp.take_along_axis(scores, topk_idx, axis=1)
            topk_w = topk_w / (topk_w.sum(-1, keepdims=True) + 1e-20)
            return (topk_idx, topk_w * SCALE)
        key = jax.random.key(seed)
        ks = jax.random.split(key, 6)
        B, S = (2, 512)
        return dict(hidden_states=jax.random.normal(ks[0], (B, S, D), jnp.float32), gate_w=jax.random.normal(ks[1], (E, D), jnp.float32) * 0.02, bias_corr=jnp.zeros((E,), jnp.float32), up_w=jax.random.normal(ks[2], (E, H, D), jnp.float32) * 0.02, down_w=jax.random.normal(ks[3], (E, D, H), jnp.float32) * 0.02, shared_up_w=jax.random.normal(ks[4], (HS, D), jnp.float32) * 0.02, shared_down_w=jax.random.normal(ks[5], (D, HS), jnp.float32) * 0.02)
    _L0_ffn_in = _L0_ffn_setup()
    _d = {'L0_attn_input_states': _L0_attn_in['input_states'], 'L0_attn_W_in': _L0_attn_in['W_in'], 'L0_attn_conv_kernel': _L0_attn_in['conv_kernel'], 'L0_attn_conv_bias': _L0_attn_in['conv_bias'], 'L0_attn_W_x': _L0_attn_in['W_x'], 'L0_attn_W_dt': _L0_attn_in['W_dt'], 'L0_attn_b_dt': _L0_attn_in['b_dt'], 'L0_attn_W_out': _L0_attn_in['W_out'], 'L0_attn_A_log': _L0_attn_in['A_log'], 'L0_attn_D': _L0_attn_in['D'], 'L0_ffn_gate_w': _L0_ffn_in['gate_w'], 'L0_ffn_bias_corr': _L0_ffn_in['bias_corr'], 'L0_ffn_up_w': _L0_ffn_in['up_w'], 'L0_ffn_down_w': _L0_ffn_in['down_w'], 'L0_ffn_shared_up_w': _L0_ffn_in['shared_up_w'], 'L0_ffn_shared_down_w': _L0_ffn_in['shared_down_w']}
    _x0 = _d['L0_attn_input_states']
    _d['L0_attn_input_states'] = jax.random.normal(jax.random.fold_in(jax.random.key(seed), 1), (4, 1024, 512), dtype=_x0.dtype)
    del _x0
    return _d

def reference(L0_attn_input_states, L0_attn_W_in, L0_attn_conv_kernel, L0_attn_conv_bias, L0_attn_W_x, L0_attn_W_dt, L0_attn_b_dt, L0_attn_W_out, L0_attn_A_log, L0_attn_D, L0_ffn_gate_w, L0_ffn_bias_corr, L0_ffn_up_w, L0_ffn_down_w, L0_ffn_shared_up_w, L0_ffn_shared_down_w):

    def _L0_attn_ref(input_states, W_in, conv_kernel, conv_bias, W_x, W_dt, b_dt, W_out, A_log, D):
        import jax, jax.numpy as jnp
        import numpy as np
        from jax import lax
        B, L, H = (2, 256, 512)
        E, N, TR, K = (1024, 16, 128, 4)
        b, l, _ = input_states.shape
        dtype = input_states.dtype
        proj = jnp.einsum('blh,he->bel', input_states, W_in)
        hidden, gate = jnp.split(proj, 2, axis=1)
        x = lax.conv_general_dilated(hidden, conv_kernel, window_strides=(1,), padding=((K - 1, K - 1),), feature_group_count=E)[..., :l]
        hidden = jax.nn.silu(x + conv_bias[None, :, None])
        hs_ble = hidden.transpose(0, 2, 1)
        ssm_p = jnp.einsum('ble,ed->bld', hs_ble, W_x)
        dt, Bm, Cm = jnp.split(ssm_p, [TR, TR + N], axis=-1)
        dts = jax.nn.softplus(jnp.einsum('blr,re->ble', dt, W_dt) + b_dt)
        A = -jnp.exp(A_log.astype(jnp.float32))
        dA = jnp.exp(dts[..., None] * A[None, None])
        dBu = dts[..., None] * Bm[:, :, None, :] * hs_ble[..., None]

        def step(state, inp):
            a, bu, c = inp
            state = a * state + bu
            y = jnp.einsum('ben,bn->be', state.astype(dtype), c)
            return (state, y)
        init = jnp.zeros((b, E, N), dtype=dtype)
        _, ys = lax.scan(step, init, (dA.transpose(1, 0, 2, 3), dBu.transpose(1, 0, 2, 3), Cm.transpose(1, 0, 2)))
        scan_out = ys.transpose(1, 2, 0)
        y = (scan_out + hidden * D[None, :, None]) * jax.nn.silu(gate)
        return jnp.einsum('bel,eh->blh', y, W_out)

    def _L0_ffn_ref(hidden_states, gate_w, bias_corr, up_w, down_w, shared_up_w, shared_down_w):
        import jax, jax.numpy as jnp
        import numpy as np
        E = 32
        G = 8
        TKG = 4
        K = 4
        D = 512
        H = 256
        HS = 1024
        SCALE = 2.5
        CAP = 256

        def relu2(x):
            r = jnp.maximum(x, 0.0)
            return r * r

        def route_tokens(scores, bias_corr):
            T = scores.shape[0]
            scores_c = scores + bias_corr
            group_scores = jax.lax.top_k(scores_c.reshape(T, G, E // G), 2)[0].sum(-1)
            _, group_idx = jax.lax.top_k(group_scores, TKG)
            group_mask = jnp.zeros((T, G), scores.dtype).at[jnp.arange(T)[:, None], group_idx].set(1.0)
            score_mask = jnp.repeat(group_mask, E // G, axis=1)
            masked = jnp.where(score_mask > 0, scores_c, 0.0)
            _, topk_idx = jax.lax.top_k(masked, K)
            topk_w = jnp.take_along_axis(scores, topk_idx, axis=1)
            topk_w = topk_w / (topk_w.sum(-1, keepdims=True) + 1e-20)
            return (topk_idx, topk_w * SCALE)
        B, S, _ = hidden_states.shape
        T = B * S
        flat = hidden_states.reshape(T, D)
        logits = flat @ gate_w.T
        scores = jax.nn.sigmoid(logits)
        topk_idx, topk_w = route_tokens(scores, bias_corr)
        e_flat = topk_idx.reshape(-1)
        oh = jax.nn.one_hot(e_flat, E, dtype=jnp.int32)
        pos = jnp.take_along_axis(jnp.cumsum(oh, axis=0) - 1, e_flat[:, None], axis=1)[:, 0]
        tok = jnp.repeat(jnp.arange(T), K)
        valid = pos < CAP
        xe = jnp.zeros((E, CAP, D), flat.dtype).at[e_flat, pos].set(flat[tok], mode='drop')
        h = relu2(jnp.einsum('ecd,ehd->ech', xe, up_w))
        ye = jnp.einsum('ech,edh->ecd', h, down_w)
        gathered = ye[e_flat, jnp.minimum(pos, CAP - 1)]
        gathered = jnp.where(valid[:, None], gathered, 0.0) * topk_w.reshape(-1)[:, None]
        routed = gathered.reshape(T, K, D).sum(axis=1).reshape(B, S, D)
        shared = relu2(hidden_states @ shared_up_w.T) @ shared_down_w.T
        return routed + shared
    x = L0_attn_input_states
    x = x + _layernorm(_L0_attn_ref(_layernorm(x, axis=-1), L0_attn_W_in, L0_attn_conv_kernel, L0_attn_conv_bias, L0_attn_W_x, L0_attn_W_dt, L0_attn_b_dt, L0_attn_W_out, L0_attn_A_log, L0_attn_D), axis=-1)
    x = x + _layernorm(_L0_ffn_ref(_layernorm(x, axis=-1), L0_ffn_gate_w, L0_ffn_bias_corr, L0_ffn_up_w, L0_ffn_down_w, L0_ffn_shared_up_w, L0_ffn_shared_down_w), axis=-1)
    return x

_drawn_inputs = setup_inputs


def setup_inputs(seed=0):
    import zlib

    import numpy as np

    out = dict(_drawn_inputs(seed))
    spreads = {'L0_ffn_bias_corr': (0.0, 0.1)}
    factors = {'L0_attn_b_dt': 3.647}
    for name, (base, spread) in spreads.items():
        noise = np.random.default_rng([zlib.crc32(name.encode()), seed]).standard_normal(out[name].shape)
        drawn = base * np.exp(spread * noise) if base else spread * noise
        out[name] = jnp.asarray(drawn.astype(out[name].dtype))
    for name, factor in factors.items():
        out[name] = (out[name] * factor).astype(out[name].dtype)
    return out
```

```python
from contextlib import ExitStack

import concourse.bass as bass
from concourse import mybir

ALU = mybir.AluOpType
ACT = mybir.ActivationFunctionType
F32 = mybir.dt.float32
I32 = mybir.dt.int32
U32 = mybir.dt.uint32
AX = mybir.AxisListType

P = 128
EPS = 1e-5
EXP_LN_SET = "natural_log_exp_and_others"

T, H, E, N, TR, TAPS, BATCH = 4096, 512, 1024, 16, 128, 4, 4
SEQ = T // BATCH
CH = 512
NCHUNK = T // CH
NPAIR = NCHUNK // 2
ET = E // P
KH = H // P
TT = CH // P
GN = 2
NG = N // GN
RING = 4
POOL_GROUPS = (3,)

NE, NGRP, TOPG, TOPK, HID, HS, CAP, SCALE = 32, 8, 4, 4, 256, 1024, 256, 2.5
GSZ = NE // NGRP
KHID, KHS = HID // P, HS // P
NTILE = T // P
FAR = 65536.0

WIN, WX, WDT = 0, KH * P, KH * P + TR + 2 * N
WPACK = WDT + P
NPAR = TAPS + 3 + N


def apart(eng):
    eng.nop(nofuse=True)


def count(value):
    return max(value, 0) if isinstance(value, int) else value


class Chunk:

    def __init__(self, pair, half):
        self.pair, self.half = pair, half

    def next(self):
        return Chunk(self.pair, 1) if self.half == 0 else Chunk(self.pair + 1, 0)

    def prev(self):
        return Chunk(self.pair, 0) if self.half == 1 else Chunk(self.pair + (-1), 1)

    def at(self, per, offset=0):
        return count(self.pair * (2 * per) + (per * self.half + offset))

    def unit(self, e):
        return self.at(ET, e)

    def group(self, e, g):
        return self.at(ET * NG, e * NG + g)

    def tile(self, j):
        return self.at(TT, j)


def run_slots(eng, slot):
    slot(None, Chunk(0, 0), None)
    slot(Chunk(0, 0), Chunk(0, 1), None)
    with eng.Fori(0, NPAIR - 1) as r:
        for now in (Chunk(r, 1), Chunk(r + 1, 0)):
            slot(now, now.next(), now.prev())
    last = Chunk(NPAIR - 1, 1)
    slot(last, None, last.prev())
    slot(None, None, last)


def copies7(ch, k, preparing):
    per, known = 3 * TT, isinstance(ch.pair, int)
    if preparing:
        if known and ch.at(1) < 2:
            return ch.at(1) * TT + k
        return ch.at(per, 2 * TT - 2 * per + k)
    if known and ch.at(1) >= NCHUNK - 2:
        return 2 * TT + per * (NCHUNK - 2) + 2 * TT * (ch.at(1) - (NCHUNK - 2)) + k
    return ch.at(per, 3 * TT + k)


def sandwich(nc, x, wpack, wgate, params, w_out, gate_t, bias_bc, sup_t, sdown_t, wexp, out,
             xe_d, ye_d, x1_d, xft_d):
    outer = ExitStack()
    with outer:
        keep_w = outer.enter_context(nc.sbuf_tensor("route_w", [P, NTILE, TOPK], F32))
        keep_slot = outer.enter_context(nc.sbuf_tensor("route_slot", [P, NTILE, TOPK], I32))
        ident = outer.enter_context(nc.sbuf_tensor("ident", [P, P], F32))
        minus_half = outer.enter_context(nc.sbuf_tensor("minus_half", [P, 1], F32))
        mixer(nc, keep_w, keep_slot, ident, minus_half, x, wpack, wgate, params, w_out, gate_t, bias_bc,
              xe_d, x1_d, xft_d)
        experts(nc, keep_w, keep_slot, ident, minus_half, sup_t, sdown_t, wexp, out,
                xe_d, ye_d, x1_d, xft_d)


def mixer(nc, keep_w, keep_slot, ident, minus_half, x, wpack, wgate, params, w_out, gate_t, bias_bc,
          xe_d, x1_d, xft_d):
    with ExitStack() as ctx:
        def sb(name, shape, dt=F32):
            return ctx.enter_context(nc.sbuf_tensor(name, shape, dt))

        def sem(name):
            return ctx.enter_context(nc.semaphore(name))

        b_bc = sb("b_bc", [P, N, CH])
        c_bc = sb("c_bc", [P, N, CH])
        hs = sb("hs", [P, ET, CH])
        gy = sb("gy", [P, 2, ET, CH])
        xnt = sb("xnt", [P, KH, CH])
        dt_t = sb("dt_t", [P, CH])
        bc_t = sb("bc_t", [2 * N, CH])
        wout_sb = sb("wout_sb", [P, ET, H])
        wp = sb("wp", [P, 2, WPACK])
        wg = sb("wg", [P, 2, KH * P])
        par = sb("par", [P, ET, NPAR])
        a_neg = par[:, :, NPAR - N:NPAR]
        diag_d = sb("diag_d", [P, 2, P])
        a_buf = sb("a_buf", [P, RING, GN, CH])
        h_buf = sb("h_buf", [P, RING, GN, CH])
        dts = sb("dts", [P, 2, CH])
        dtu = sb("dtu", [P, 2, CH])
        tail = sb("tail", [P, ET, TAPS - 1])
        state = sb("state", [P, ET, N])
        x_in = sb("x_in", [P, 2, H])
        x1 = sb("x1", [P, H])
        xf = sb("xf", [P, TT, H])
        xft = sb("xft", [P, KH * P])
        gate_sb = sb("gate_sb", [P, KH, NE])
        bias_sb = sb("bias_sb", [P, NE])
        before = sb("before", [P, P])
        ones = sb("ones", [P, P])
        st = sb("st", [P, 3, 6])
        mv = sb("mv", [P, 3, 2])
        rstd = sb("rstd", [P, 3])
        score = sb("score", [P, TT, NE])
        biased = sb("biased", [P, TT, NE])
        r_a = sb("r_a", [P, TT * NGRP, 2])
        r_b = sb("r_b", [P, TT * NGRP, 2])
        r_c = sb("r_c", [P, 3, TT * NGRP])
        gsum = sb("gsum", [P, TT, NGRP])
        cmp = xft[:, 0:TT * NGRP * NGRP].rearrange("p (j g h) -> p j g h", j=TT, g=NGRP)
        cmp2 = xft[:, TT * NGRP * NGRP:].rearrange("p (j g h) -> p j g h", j=TT, g=NGRP)
        earlier = sb("earlier", [P, NGRP, NGRP])
        rank = sb("rank", [P, TT, NGRP])
        top_v = sb("top_v", [P, TT, 8])
        top_i = sb("top_i", [P, TT, 8], U32)
        idx_f = sb("idx_f", [P, TT, TOPK])
        one_hot = x_in[:, 0, :].rearrange("p (j k e) -> p j k e", j=TT, k=TOPK)
        picked = x_in[:, 1, :].rearrange("p (j k e) -> p j k e", j=TT, k=TOPK)
        chosen = sb("chosen", [P, TT, NE])
        wtmp = sb("wtmp", [P, TT, TOPK])
        valid = sb("valid", [P, TT, TOPK])
        slot_now = sb("slot_now", [P, TT, TOPK], I32)
        iota_i = sb("iota_i", [P, NE], I32)
        iota_f = sb("iota_f", [P, NE])
        pos_all = biased
        base = sb("base", [P, NE])
        pos = sb("pos", [P, TT, TOPK])
        slot_f = sb("slot_f", [P, TT, TOPK])
        wsum = sb("wsum", [P, TT])

        def bank(name):
            return ctx.enter_context(nc.psum_tensor(name, [P, 512], F32))

        hid_p, gate_p, dtacc_p, bcacc_p, dts_p = (bank(f"{n}_p") for n in ("hid", "gt", "dta", "bca", "dts"))
        y_p = [bank("y0_p"), bank("y1_p")]
        misc_p = bank("misc_p")
        wide_p = (dtacc_p, bcacc_p)

        s_par = sem("params_loaded")
        s_const = sem("const_loaded")
        s_w = [sem("wpack0_loaded"), sem("wpack1_loaded")]
        s_wg = [sem("wgate0_loaded"), sem("wgate1_loaded")]
        s_x = [sem("x_in0_loaded"), sem("x_in1_loaded")]
        s_x1 = sem("x1_loaded")
        s_x1_out = sem("x1_stored")
        s_xft_out = sem("xft_stored")
        s_zero = sem("slots_zeroed")
        s_scat = sem("rows_scattered")
        g_setup = sem("pool_setup")
        v_setup = sem("dve_setup")
        a_setup = sem("act_setup")
        v_ln1 = sem("ln1_steps")
        g_ln1 = sem("ln1_rstd")
        t_ln1 = sem("ln1_transposed")
        t_hid = sem("hidden_projected")
        t_gp = sem("gate_projected")
        a_tap = sem("tap_done")
        v_conv = sem("conv_steps")
        a_hs = sem("hidden_silu")
        a_gs = sem("gate_silu")
        t_wx = sem("wx_done")
        a_dtbc = sem("dt_bc_copied")
        t_bc = sem("bc_spread")
        a_bc = sem("bc_copied")
        t_dts = sem("dt_projected")
        v_clamp = sem("dt_clamped")
        a_sp = sem("softplus_steps")
        v_dts = sem("dts_ready")
        v_dtu = sem("dtu_ready")
        a_exp = sem("decay_ready")
        g_diag = sem("diagonal_ready")
        g_dbu = sem("input_ready")
        v_scan = sem("scanned")
        v_keep = sem("states_kept")
        v_cp = sem("c_product_dve")
        g_cp = sem("c_product_pool")
        t_sum = sem("states_summed")
        v_y = sem("y_ready")
        t_out = sem("w_out_done")
        v_c = sem("finish_steps")
        g_c = sem("finish_rstd")
        t_xft = sem("xf_transposed")
        t_gate = sem("gate_done")
        v_r = sem("route_steps")
        t_pos = sem("pos_counted")
        a_c7 = sem("bank7_copied")

        NDVE = NG - len(POOL_GROUPS)

        def c_count(e_ch, e, g):
            mine = [q for q in range(g + 1) if q in POOL_GROUPS]
            return (e_ch.at(ET * NDVE, e * NDVE + g + 1 - len(mine)),
                    e_ch.at(ET * len(POOL_GROUPS), e * len(POOL_GROUPS) + len(mine)))

        def wait_c_product(eng, ch, e, g):
            dve, pool = c_count(ch, e, g)
            if g in POOL_GROUPS:
                eng.wait_ge(g_cp, pool)
            else:
                eng.wait_ge(v_cp, dve)

        def wait_kept(eng, ch, e, g):
            if ch.half == 0:
                eng.wait_ge(v_keep, ch.pair * (ET * NG) + (e * NG + g + 1))

        def conv_count(ch, e, done):
            per = (2 * (TAPS - 1)) if ch.half else (TAPS - 1)
            return ch.pair * (ET * 3 * (TAPS - 1)) + (ch.half * ET * (TAPS - 1) + e * per + done)

        def conv_all(ch, e):
            return conv_count(ch, e, 2 * (TAPS - 1) if ch.half else TAPS - 1)

        x_tiles = x.rearrange("(i p) h -> i p h", p=P)
        x1_tiles = x1_d.rearrange("(i p) h -> i p h", p=P)
        R, R_CHOSEN, R_POS = 46, 28, 36

        block = ctx.enter_context(nc.Block())

        @block.sync
        def _(sp):
            def load_pack(v, e, freed_by, count):
                sp.wait_ge(freed_by, count)
                sp.dma_start(wp[:, e % 2, :], wpack[e]).then_inc(s_w[e % 2], 16)

            def load_gate(ch, e):
                sp.wait_ge(t_gp, ch.unit(e - 1))
                sp.dma_start(wg[:, e % 2, :], wgate[e]).then_inc(s_wg[e % 2], 16)

            def tile_of(dram, i):
                return dram[bass.ds(i, 1), :, :].rearrange("a p h -> (a p) h")

            def load_x(ch, j):
                sp.wait_ge(t_ln1, ch.tile(j - 1))
                apart(sp)
                sp.wait_ge(v_r, ch.at(R, -2 * R))
                apart(sp)
                sp.dma_start(x_in[:, j % 2, :], tile_of(x_tiles, ch.tile(j))).then_inc(s_x[j % 2], 16)

            def load_x1(ch, j):
                sp.wait_ge(s_x1_out, ch.at(16 * TT, 16 * j))
                apart(sp)
                sp.wait_ge(v_c, ch.at(7 * TT, 7 * j))
                apart(sp)
                sp.dma_start(x1[:], tile_of(x_tiles, ch.tile(j))).then_inc(s_x1, 16)

            def store_x1(ch, j):
                sp.wait_ge(v_c, ch.at(7 * TT, 7 * j + 4))
                sp.dma_start(tile_of(x1_tiles, ch.tile(j)), x1[:]).then_inc(s_x1_out, 16)

            def store_xft(ch, j):
                sp.wait_ge(a_c7, copies7(ch, 2 * j, False) + 1)
                sp.dma_start(xft_d[bass.ds(ch.tile(j), 1), :, :].rearrange("a p c -> (a p) c"),
                             xft[:]).then_inc(s_xft_out, 16)

            sp.dma_start(par[:], params).then_inc(s_par, 16)

            def slot(now, ready, done):
                if ready is not None:
                    for j in range(TT):
                        load_x(ready, j)
                        if now is None and j == 1:
                            for e in range(2):
                                load_pack(e, e, t_wx, 0)
                            sp.dma_start(wout_sb[:], w_out).then_inc(s_const, 16)
                            sp.dma_start(gate_sb[:], gate_t).then_inc(s_const, 16)
                            sp.dma_start(bias_sb[:], bias_bc).then_inc(s_const, 16)
                for e in range(ET):
                    if done is not None and 1 <= e <= TT:
                        store_xft(done, e - 1)
                    if done is not None and e < TT:
                        load_x1(done, e)
                    if now is None and ready is not None:
                        load_gate(ready, e)
                        load_pack(e + 2, (e + 2) % ET, t_wx, e + 1)
                    elif ready is not None:
                        for q in (2 * e + 2 - ET, 2 * e + 3 - ET):
                            if 0 <= q < ET:
                                load_gate(ready, q)
                        load_pack(now.unit(ET + e + 2), (e + 2) % ET, t_wx, now.unit(ET + e + 1))
                    elif now is not None and e + 2 < ET:
                        load_pack(now.unit(ET + e + 2), e + 2, t_dts, now.unit(e + 1))
                    if done is not None and e < TT:
                        store_x1(done, e)

            run_slots(sp, slot)
            sp.wait_ge(s_x1_out, 16 * NTILE)
            sp.wait_ge(s_xft_out, 16 * NTILE)
            sp.wait_ge(s_scat, 16 * NTILE * TOPK)

        @block.gpsimd
        def _(pool):
            setup = [0]

            def step(ins):
                setup[0] += 1
                ins.then_inc(g_setup, 1)

            step(nc.gpsimd.memset(ident[:], 0.0))
            step(nc.gpsimd.memset(xf[:, 0, :], 0.0))
            step(nc.gpsimd.memset(ones[:], 1.0))
            step(nc.gpsimd.memset(before[:], 1.0))
            step(nc.gpsimd.memset(earlier[:], 1.0))
            step(nc.gpsimd.memset(minus_half[:], -0.5))
            step(nc.gpsimd.iota(iota_i[:], pattern=[[1, NE]], base=0, channel_multiplier=0))
            pool.wait_ge(g_setup, 7)
            step(nc.gpsimd.affine_select(out=ident[:], in_=ident[:], compare_op=ALU.not_equal, fill=1.0,
                                         base=0, pattern=[[-1, P]], channel_multiplier=1))
            step(nc.gpsimd.affine_select(out=before[:], in_=before[:], compare_op=ALU.is_gt, fill=0.0,
                                         base=0, pattern=[[1, P]], channel_multiplier=-1))
            step(nc.gpsimd.affine_select(out=earlier[:], in_=earlier[:], compare_op=ALU.is_gt, fill=0.0,
                                         base=0, pattern=[[1, NGRP], [-1, NGRP]], channel_multiplier=0))
            step(nc.gpsimd.tensor_copy(iota_f[:], iota_i[:]))
            pool.wait_ge(g_setup, 11)
            pool.wait_ge(s_par, 16)

            def diagonal(ch, e):
                pool.wait_ge(t_sum, ch.at(ET * NG, NG * (e - 2) + 1))
                apart(pool)
                nc.gpsimd.tensor_scalar(diag_d[:, e % 2, :], ident[:], par[:, e, TAPS + 2:TAPS + 3], None,
                                        ALU.mult).then_inc(g_diag, 1)

            def input_term(ch, e, g):
                u, q = ch.unit(e), ch.group(e, g)
                if g == 0:
                    pool.wait_ge(v_dtu, ch.unit(e + 1))
                if e == 0:
                    pool.wait_ge(a_bc, ch.at(2 * N, 4 * g + 2))
                pool.wait_ge(t_sum, ch.group(e, g + 1 - RING))
                nc.gpsimd.tensor_tensor(
                    h_buf[:, g % RING], dtu[:, e % 2, :].unsqueeze(1).to_broadcast((P, GN, CH)),
                    b_bc[:, g * GN:(g + 1) * GN, :], ALU.mult).then_inc(g_dbu, 1)

            def c_product(ch, e, g):
                pool.wait_ge(v_scan, ch.at(ET * N, e * N + (g + 1) * GN))
                wait_kept(pool, ch, e, g)
                if e == 0:
                    pool.wait_ge(a_bc, ch.at(2 * N, 4 * g + 4))
                nc.gpsimd.tensor_tensor(h_buf[:, g % RING], h_buf[:, g % RING],
                                        c_bc[:, g * GN:(g + 1) * GN, :], ALU.mult).then_inc(g_cp, 1)

            def rstd_of(k, sem_in, count_in, sem_out, count_out):
                pool.wait_ge(sem_in, count_in)
                apart(pool)
                nc.gpsimd.tensor_scalar(rstd[:, k:k + 1], mv[:, k, 1:2], EPS, None, ALU.add).then_inc(sem_out, 1)
                pool.wait_ge(sem_out, count_out)
                nc.gpsimd.tensor_tensor(rstd[:, k:k + 1], rstd[:, k:k + 1], minus_half[:], ALU.pow
                                        ).then_inc(sem_out, 1)

            def prepare_norm(ch, j):
                rstd_of(0, v_ln1, ch.at(3 * TT, 3 * j + 2), g_ln1, ch.at(2 * TT, 2 * j + 1))

            def finish_norm(ch, j, k):
                rstd_of(1 + k, v_c, ch.at(7 * TT, 7 * j + 2 + 4 * k), g_c, ch.at(4 * TT, 4 * j + 2 * k + 1))

            def scatter(ch, m):
                j, k = m // TOPK, m % TOPK
                if m == 0:
                    pool.wait_ge(v_r, ch.at(R, R))
                    pool.wait_ge(s_zero, 16)
                apart(pool)
                nc.gpsimd.indirect_dma_start(
                    xe_d, bass.IndirectOffsetOnAxis(ap=slot_now[:, j, k:k + 1].bitcast(U32), axis=0),
                    xf[:, j, :], None, bounds_check=NE * CAP - 1, oob_is_err=False).then_inc(s_scat, 16)

            def slot(now, ready, done):
                if now is None:
                    if ready is not None:
                        for j in range(TT):
                            prepare_norm(ready, j)
                    if done is not None:
                        for j in range(TT):
                            finish_norm(done, j, 0)
                            finish_norm(done, j, 1)
                        for m in range(TT * TOPK):
                            scatter(done, m)
                    return
                for e in range(ET):
                    diagonal(now, e)
                    for g in range(NG):
                        if g - 2 in POOL_GROUPS:
                            c_product(now, e, g - 2)
                        input_term(now, e, g)
                        if ready is not None and e == 0 and 1 <= g <= TT:
                            prepare_norm(ready, g - 1)
                        if done is not None:
                            if 1 <= e <= TT and g == 1:
                                finish_norm(done, e - 1, 0)
                            if 1 <= e <= TT and g == 3:
                                finish_norm(done, e - 1, 1)
                        if done is not None and e >= 6:
                            scatter(done, (e - 6) * NG + g)

            run_slots(pool, slot)

        @block.scalar
        def _(act):
            act.wait_ge(g_setup, 2)
            act.dma_start(xe_d.rearrange("(p r) h -> p r h", p=P),
                          xf[:, 0, :].unsqueeze(1).to_broadcast((P, NE * CAP // P, H))).then_inc(s_zero, 16)
            nc.scalar.preload_act_table_set(EXP_LN_SET)
            act.wait_ge(s_par, 16)
            nc.scalar.activation(a_neg, a_neg, ACT.Exp).then_inc(a_setup, 1)
            act.wait_ge(a_setup, 1)
            nc.scalar.mul(a_neg, a_neg, -1.0).then_inc(a_setup, 1)
            act.wait_ge(a_setup, 2)

            def xnt_copy(ch, j):
                act.wait_ge(t_ln1, ch.tile(j + 1))
                if j == 0:
                    act.wait_ge(t_hid, ch.unit(0))
                    act.wait_ge(t_gp, ch.unit(0))
                nc.scalar.copy(xnt[:, :, j * P:(j + 1) * P],
                               misc_p[:].rearrange("p (k t) -> p k t", k=KH)).then_inc(a_c7, 1)

            def last_tap(ch, e):
                act.wait_ge(t_hid, ch.unit(e + 1))
                if not first(ch):
                    act.wait_ge(v_dtu, ch.at(ET, e + 1 - ET))
                    act.wait_ge(t_sum, ch.at(ET * NG, (e - ET) * NG + 1))
                ins = nc.scalar.activation(hs[:, e, :], hid_p[:], ACT.Identity, scale=par[:, e, TAPS - 1:TAPS],
                                           bias=par[:, e, TAPS:TAPS + 1])
                if ch.half == 0:
                    if e == 0:
                        act.wait_ge(v_conv, conv_count(ch, 0, 0))
                    ins = nc.scalar.copy(tail[:, e, :], hid_p[:, CH - TAPS + 1:CH])
                ins.then_inc(a_tap, 1)

            def silu_hidden(ch, e):
                act.wait_ge(v_conv, conv_all(ch, e))
                nc.scalar.activation(hs[:, e, :], hs[:, e, :], ACT.Silu).then_inc(a_hs, 1)

            def silu_gate(ch, e):
                act.wait_ge(t_gp, ch.unit(e + 1))
                if e == 0:
                    act.wait_ge(t_out, ch.at(TT, -TT))
                nc.scalar.activation(gy[:, ch.half, e, :], gate_p[:], ACT.Silu).then_inc(a_gs, 1)

            def first(ch):
                return isinstance(ch.pair, int) and ch.at(1) == 0

            def dt_bc_copy(ch):
                act.wait_ge(t_wx, ch.at(ET, ET))
                act.wait_ge(t_dts, ch.at(ET, 0))
                nc.scalar.copy(dt_t[:], dtacc_p[:]).then_inc(a_dtbc, 1)
                act.wait_ge(t_bc, ch.at(2 * N, 0))
                nc.scalar.copy(bc_t[:], bcacc_p[0:2 * N, :]).then_inc(a_dtbc, 1)

            def spread(ch, g):
                for k in range(4):
                    m = 4 * g + k
                    n = g * GN + k % 2
                    act.wait_ge(t_bc, ch.at(2 * N, m + 1))
                    if not first(ch):
                        if k == 0:
                            act.wait_ge(g_dbu, ch.at(ET * NG, g + 1 - NG))
                        if k == 2:
                            wait_c_product(act, ch.prev(), ET - 1, g)
                    nc.scalar.copy((b_bc if k < 2 else c_bc)[:, n, :], wide_p[m % 2][:]).then_inc(a_bc, 1)

            def softplus(ch, e):
                b = e % 2
                act.wait_ge(v_clamp, ch.unit(e + 1))
                nc.scalar.activation(dts[:, b, :], dts[:, b, :], ACT.Exp).then_inc(a_sp, 1)
                act.wait_ge(a_sp, ch.at(2 * ET, 2 * e + 1))
                nc.scalar.activation(dts[:, b, :], dts[:, b, :], ACT.Ln, bias=1.0).then_inc(a_sp, 1)

            def decay(ch, e, g):
                if g == 0:
                    act.wait_ge(v_dts, ch.unit(e + 1))
                act.wait_ge(v_scan, ch.at(ET * N, e * N + (g + 1 - RING) * GN))
                for k in range(GN):
                    n = g * GN + k
                    ins = nc.scalar.activation(a_buf[:, g % RING, k, :], dts[:, e % 2, :], ACT.Exp,
                                               scale=a_neg[:, e, n:n + 1])
                ins.then_inc(a_exp, 1)

            def xft_copy(ch, j):
                act.wait_ge(t_xft, ch.tile(j + 1))
                act.wait_ge(s_xft_out, ch.at(16 * TT, 16 * j))
                act.wait_ge(t_gate, ch.tile(j))
                act.wait_ge(v_r, ch.at(R, 0))
                nc.scalar.copy(xft[:], misc_p[:]).then_inc(a_c7, 1)

            def gate_exp(ch, j):
                act.wait_ge(t_gate, ch.tile(j + 1))
                nc.scalar.activation(score[:, j, :], misc_p[:, 0:NE], ACT.Exp, scale=-1.0).then_inc(a_c7, 1)

            def slot(now, ready, done):
                if now is None and ready is not None:
                    for j in range(TT):
                        xnt_copy(ready, j)
                    for e in range(ET):
                        last_tap(ready, e)
                        silu_gate(ready, e)
                        silu_hidden(ready, e)
                    nc.scalar.preload_act_table_set(EXP_LN_SET)
                    dt_bc_copy(ready)
                    softplus(ready, 0)
                    return
                if now is None:
                    for j in range(TT):
                        xft_copy(done, j)
                        gate_exp(done, j)
                    return
                for e in range(ET):
                    for g in range(NG):
                        if e == 0:
                            spread(now, g)
                        decay(now, e, g)
                        if done is not None and 1 <= e <= TT:
                            if g == 5:
                                xft_copy(done, e - 1)
                            if g == 6:
                                gate_exp(done, e - 1)
                        if ready is not None:
                            if e == 0 and 1 <= g <= TT:
                                xnt_copy(ready, g - 1)
                            if g == (6 if e == 0 else 1):
                                last_tap(ready, e)
                            if e >= ET // 2 and g == 2:
                                silu_gate(ready, 2 * (e - ET // 2))
                            if g == (7 if e == 0 else 3):
                                silu_hidden(ready, e)
                                if e >= ET // 2:
                                    silu_gate(ready, 2 * (e - ET // 2) + 1)
                                nc.scalar.preload_act_table_set(EXP_LN_SET)
                            if e == ET - 1 and g == 5:
                                dt_bc_copy(ready)
                            if e == ET - 1 and g == 6:
                                softplus(ready, 0)
                        if e < ET - 1 and g == 6:
                            softplus(now, e + 1)

            run_slots(act, slot)

        @block.tensor
        def _(pe):
            pe.wait_ge(g_setup, 11)
            transpose = nc.tensor.transpose

            def ln1_transpose(ch, j):
                pe.wait_ge(v_ln1, ch.at(3 * TT, 3 * j + 3))
                pe.wait_ge(a_c7, copies7(ch, j, True))
                for k in range(KH):
                    mm = transpose(misc_p[:, k * P:(k + 1) * P], x_in[:, j % 2, k * P:(k + 1) * P], ident[:])
                mm.then_inc(t_ln1, 1)

            def project(ch, e):
                pe.wait_ge(s_w[e % 2], ch.at(16 * ET // 2, 16 * (e // 2 + 1)))
                if e == 0:
                    pe.wait_ge(a_c7, copies7(ch, TT - 1, True) + 1)
                pe.wait_ge(a_tap, ch.unit(e))
                pe.wait_ge(v_conv, conv_all(ch, e - 1) if e else conv_count(ch, 0, 0))
                for k in range(KH):
                    mm = nc.tensor.matmul(hid_p[:], wp[:, e % 2, WIN + k * P:WIN + (k + 1) * P], xnt[:, k, :],
                                          start=(k == 0), stop=(k == KH - 1))
                mm.then_inc(t_hid, 1)

            def project_gate(ch, e):
                pe.wait_ge(s_wg[e % 2], ch.at(16 * ET // 2, 16 * (e // 2 + 1)))
                pe.wait_ge(a_gs, ch.unit(e))
                for k in range(KH):
                    mm = nc.tensor.matmul(gate_p[:], wg[:, e % 2, k * P:(k + 1) * P],
                                          xnt[:, k, :], start=(k == 0), stop=(k == KH - 1))
                mm.then_inc(t_gp, 1)

            def project_x(ch, e):
                pe.wait_ge(a_hs, ch.unit(e + 1))
                if e == 0:
                    pe.wait_ge(a_bc, ch.at(2 * N, 0))
                nc.tensor.matmul(dtacc_p[:], wp[:, e % 2, WX:WX + TR], hs[:, e, :],
                                 start=(e == 0), stop=(e == ET - 1))
                nc.tensor.matmul(bcacc_p[0:2 * N, :], wp[:, e % 2, WX + TR:WX + TR + 2 * N], hs[:, e, :],
                                 start=(e == 0), stop=(e == ET - 1)).then_inc(t_wx, 1)

            def spread(ch, g):
                for k in range(4):
                    m = 4 * g + k
                    row = (0 if k < 2 else N) + g * GN + k % 2
                    if m < 2:
                        pe.wait_ge(a_dtbc, ch.at(2, 2))
                    else:
                        pe.wait_ge(a_bc, ch.at(2 * N, m - 1))
                    nc.tensor.matmul(wide_p[m % 2][:], ident[0:2 * N, row:row + 1].to_broadcast((2 * N, P)),
                                     bc_t[:], start=True, stop=True).then_inc(t_bc, 1)

            def project_dt(ch, e):
                if e == 0:
                    pe.wait_ge(a_dtbc, ch.at(2, 1))
                pe.wait_ge(s_w[e % 2], ch.at(16 * ET // 2, 16 * (ET // 2) + 16 * (e // 2 + 1)))
                pe.wait_ge(v_dts, ch.unit(e))
                nc.tensor.matmul(dts_p[:], wp[:, e % 2, WDT:WDT + P], dt_t[:],
                                 start=True, stop=True).then_inc(t_dts, 1)

            def skip_term(ch, e):
                pe.wait_ge(v_y, ch.unit(e - 1))
                pe.wait_ge(g_diag, ch.unit(e + 1))
                nc.tensor.matmul(y_p[e % 2][:], diag_d[:, e % 2, :], hs[:, e, :], start=True, stop=False)

            def sum_states(ch, e, g):
                wait_c_product(pe, ch, e, g)
                for k in range(GN):
                    mm = nc.tensor.matmul(y_p[e % 2][:], ident[:], h_buf[:, g % RING, k, :], start=False,
                                          stop=(g == NG - 1 and k == GN - 1))
                mm.then_inc(t_sum, 1)

            def project_out(ch, j):
                pe.wait_ge(v_y, ch.unit(ET))
                pe.wait_ge(a_c7, copies7(ch, 2 * j, False))
                for k in range(ET):
                    mm = nc.tensor.matmul(misc_p[:], gy[:, ch.half, k, j * P:(j + 1) * P], wout_sb[:, k, :],
                                          start=(k == 0), stop=(k == ET - 1))
                mm.then_inc(t_out, 1)

            def xf_transpose(ch, j):
                pe.wait_ge(v_c, ch.at(7 * TT, 7 * j + 7))
                for k in range(KH):
                    mm = transpose(misc_p[:, k * P:(k + 1) * P], xf[:, j, k * P:(k + 1) * P], ident[:])
                mm.then_inc(t_xft, 1)

            def gate_logits(ch, j):
                pe.wait_ge(a_c7, copies7(ch, 2 * j, False) + 1)
                for k in range(KH):
                    mm = nc.tensor.matmul(misc_p[:, 0:NE], xft[:, k * P:(k + 1) * P], gate_sb[:, k, :],
                                          start=(k == 0), stop=(k == KH - 1))
                mm.then_inc(t_gate, 1)

            def count_positions(ch):
                pe.wait_ge(v_r, ch.at(R, R_CHOSEN))
                pe.wait_ge(a_c7, copies7(ch, 2 * TT - 1, False) + 1)
                for j in range(TT):
                    for i in range(j + 1):
                        nc.tensor.matmul(misc_p[:, j * NE:(j + 1) * NE], (before if i == j else ones)[:],
                                         chosen[:, i, :], start=(i == 0), stop=(i == j))
                for i in range(TT):
                    mm = nc.tensor.matmul(misc_p[:, TT * NE:(TT + 1) * NE], ones[:], chosen[:, i, :],
                                          start=(i == 0), stop=(i == TT - 1))
                mm.then_inc(t_pos, 1)

            def slot(now, ready, done):
                if now is None and ready is not None:
                    for j in range(TT):
                        ln1_transpose(ready, j)
                    for e in range(ET):
                        project(ready, e)
                        project_gate(ready, e)
                        project_x(ready, e)
                    project_dt(ready, 0)
                    pe.wait_ge(s_const, 48)
                    return
                if now is None:
                    for j in range(TT):
                        project_out(done, j)
                        xf_transpose(done, j)
                        gate_logits(done, j)
                    count_positions(done)
                    return
                for e in range(ET):
                    skip_term(now, e)
                    for g in range(NG):
                        if e == 0:
                            if ready is not None and 1 <= g <= TT:
                                ln1_transpose(ready, g - 1)
                            for q in range(g + (g > 0), min(g + 2, NG)):
                                spread(now, q)
                        if done is not None:
                            if 1 <= e <= TT and g == 6:
                                gate_logits(done, e - 1)
                            if e < TT and g == 6:
                                project_out(done, e)
                            if e == 5 and g == 3:
                                count_positions(done)
                        if ready is not None:
                            if e == 1 and g == 0:
                                project_x(ready, 0)
                            if g == (5 if e == 0 else 0):
                                project(ready, e)
                            if e >= ET // 2 and g in (1, 2):
                                project_gate(ready, 2 * (e - ET // 2) + g - 1)
                            if e > 0 and g == 4:
                                project_x(ready, e)
                            if e == ET - 1 and g == 5:
                                project_dt(ready, 0)
                        if e < ET - 1 and g == 5:
                            project_dt(now, e + 1)
                        sum_states(now, e, g)
                        if done is not None and 1 <= e <= TT and g == 4:
                            xf_transpose(done, e - 1)

            run_slots(pe, slot)

        @block.vector
        def _(dve):
            V = nc.vector
            V.memset(base[:], 0.0).then_inc(v_setup, 1)
            dve.wait_ge(v_setup, 1)
            dve.wait_ge(g_setup, 11)
            dve.wait_ge(s_par, 16)

            def prepare_stats(ch, j):
                dve.wait_ge(s_x[j % 2], ch.at(8 * TT, 16 * (j // 2 + 1)))
                V.bn_stats(st[:, 0, :], x_in[:, j % 2, :]).then_inc(v_ln1, 1)
                dve.wait_ge(v_ln1, ch.at(3 * TT, 3 * j + 1))
                dve.wait_ge(g_ln1, ch.at(2 * TT, 2 * j))
                apart(dve)
                V.bn_aggr(mv[:, 0, :], st[:, 0, :]).then_inc(v_ln1, 1)

            def prepare_norm(ch, j):
                dve.wait_ge(g_ln1, ch.at(2 * TT, 2 * j + 2))
                V.tensor_scalar(x_in[:, j % 2, :], x_in[:, j % 2, :], mv[:, 0, 0:1], rstd[:, 0:1],
                                ALU.subtract, ALU.mult).then_inc(v_ln1, 1)

            def convolve(ch, e):
                dve.wait_ge(a_tap, ch.unit(e + 1))
                n = 0
                for s in range(1, TAPS):
                    tap = par[:, e, TAPS - 1 - s:TAPS - s]
                    if n:
                        dve.wait_ge(v_conv, conv_count(ch, e, n))
                    V.scalar_tensor_tensor(hs[:, e, s:], hid_p[:, 0:CH - s], tap, hs[:, e, s:],
                                           op0=ALU.mult, op1=ALU.add).then_inc(v_conv, 1)
                    n += 1
                    if ch.half:
                        dve.wait_ge(v_conv, conv_count(ch, e, n))
                        V.scalar_tensor_tensor(hs[:, e, 0:s], tail[:, e, TAPS - 1 - s:], tap, hs[:, e, 0:s],
                                               op0=ALU.mult, op1=ALU.add).then_inc(v_conv, 1)
                        n += 1

            def clamp_dt(ch, e):
                b = e % 2
                dve.wait_ge(t_dts, ch.unit(e + 1))
                dve.wait_ge(a_exp, ch.group(e - 1, 0))
                V.tensor_scalar(dts[:, b, :], dts_p[:], par[:, e, TAPS + 1:TAPS + 2], 40.0,
                                ALU.add, ALU.min).then_inc(v_clamp, 1)

            def finish_dt(ch, e):
                b = e % 2
                dve.wait_ge(a_sp, ch.at(2 * ET, 2 * e + 2))
                V.scalar_tensor_tensor(dts[:, b, :], dts_p[:], par[:, e, TAPS + 1:TAPS + 2], dts[:, b, :],
                                       op0=ALU.add, op1=ALU.max).then_inc(v_dts, 1)
                dve.wait_ge(v_dts, ch.unit(e + 1))
                dve.wait_ge(a_hs, ch.unit(e + 1))
                dve.wait_ge(g_dbu, ch.group(e - 1, 0))
                V.tensor_tensor(dtu[:, b, :], dts[:, b, :], hs[:, e, :], ALU.mult).then_inc(v_dtu, 1)

            def scan(ch, e, g):
                dve.wait_ge(g_dbu, ch.group(e, g + 1))
                dve.wait_ge(a_exp, ch.group(e, g + 1))
                if ch.half:
                    wait_kept(dve, ch.prev(), e, g)
                for k in range(GN):
                    n = g * GN + k
                    V.tensor_tensor_scan(h_buf[:, g % RING, k, :], a_buf[:, g % RING, k, :],
                                         h_buf[:, g % RING, k, :],
                                         state[:, e, n:n + 1] if ch.half else 0.0,
                                         ALU.mult, ALU.add).then_inc(v_scan, 1)

            def keep_state(ch, e, g):
                if ch.half == 0:
                    dve.wait_ge(v_scan, ch.at(ET * N, e * N + (g + 1) * GN))
                    V.tensor_copy(state[:, e, g * GN:(g + 1) * GN], h_buf[:, g % RING, :, CH - 1]
                                  ).then_inc(v_keep, 1)

            def c_product(ch, e, g):
                dve.wait_ge(v_scan, ch.at(ET * N, e * N + (g + 1) * GN))
                wait_kept(dve, ch, e, g)
                if e == 0:
                    dve.wait_ge(a_bc, ch.at(2 * N, 4 * g + 4))
                V.tensor_tensor(h_buf[:, g % RING], h_buf[:, g % RING],
                                c_bc[:, g * GN:(g + 1) * GN, :], ALU.mult).then_inc(v_cp, 1)

            def gate_y(ch, e):
                dve.wait_ge(t_sum, ch.group(e + 1, 0))
                dve.wait_ge(a_gs, ch.unit(e + 1))
                V.tensor_tensor(gy[:, ch.half, e, :], y_p[e % 2][:], gy[:, ch.half, e, :],
                                ALU.mult).then_inc(v_y, 1)

            def finish_step(ch, j, n, ins):
                ins.then_inc(v_c, 1)
                dve.wait_ge(v_c, ch.at(7 * TT, 7 * j + n))

            def finish_stats(ch, j):
                dve.wait_ge(t_out, ch.tile(j + 1))
                finish_step(ch, j, 1, V.bn_stats(st[:, 1, :], misc_p[:]))
                dve.wait_ge(g_c, ch.at(4 * TT, 4 * j))
                apart(dve)
                finish_step(ch, j, 2, V.bn_aggr(mv[:, 1, :], st[:, 1, :]))

            def finish_add(ch, j):
                dve.wait_ge(g_c, ch.at(4 * TT, 4 * j + 2))
                if j == 0:
                    dve.wait_ge(s_scat, ch.at(16 * TT * TOPK, 0))
                    dve.wait_ge(s_zero, 16)
                finish_step(ch, j, 3, V.tensor_scalar(xf[:, j, :], misc_p[:], mv[:, 1, 0:1], rstd[:, 1:2],
                                                      ALU.subtract, ALU.mult))
                dve.wait_ge(s_x1, ch.at(16 * TT, 16 * (j + 1)))
                finish_step(ch, j, 4, V.tensor_tensor(x1[:], x1[:], xf[:, j, :], ALU.add))
                finish_step(ch, j, 5, V.bn_stats(st[:, 2, :], x1[:]))
                apart(dve)
                finish_step(ch, j, 6, V.bn_aggr(mv[:, 2, :], st[:, 2, :]))

            def finish_norm(ch, j):
                dve.wait_ge(g_c, ch.at(4 * TT, 4 * j + 4))
                V.tensor_scalar(xf[:, j, :], x1[:], mv[:, 2, 0:1], rstd[:, 2:3],
                                ALU.subtract, ALU.mult).then_inc(v_c, 1)

            def route(ch, part):
                made = [0 if part == 0 else R_POS - 1]

                def step(ins):
                    made[0] += 1
                    ins.then_inc(v_r, 1)
                    dve.wait_ge(v_r, ch.at(R, made[0]))

                def over_k(a):
                    return a.unsqueeze(2).to_broadcast((P, TT, TOPK, NE))

                def flat(a):
                    return a.rearrange("p j k e -> p (j k) e")

                if part == 0:
                    dve.wait_ge(a_c7, copies7(ch, 2 * TT - 1, False) + 1)
                    dve.wait_ge(s_xft_out, ch.at(16 * TT, 16 * TT))
                    step(V.tensor_scalar(score[:], score[:], 1.0, None, ALU.add))
                    step(V.reciprocal(score[:], score[:]))
                    step(V.tensor_tensor(biased[:], score[:], bias_sb[:].unsqueeze(1).to_broadcast((P, TT, NE)),
                                         ALU.add))
                    pairs = biased[:].rearrange("p j (q two) -> p (j q) two", two=2)
                    step(V.tensor_tensor(r_a[:].rearrange("p q two -> p (q two)"), pairs[:, :, 0], pairs[:, :, 1],
                                         ALU.max))
                    step(V.tensor_tensor(r_b[:].rearrange("p q two -> p (q two)"), pairs[:, :, 0], pairs[:, :, 1],
                                         ALU.min))
                    step(V.tensor_tensor(r_c[:, 0, :], r_a[:, :, 0], r_a[:, :, 1], ALU.max))
                    step(V.tensor_tensor(r_c[:, 1, :], r_a[:, :, 0], r_a[:, :, 1], ALU.min))
                    step(V.tensor_tensor(r_c[:, 2, :], r_b[:, :, 0], r_b[:, :, 1], ALU.max))
                    step(V.tensor_tensor(r_c[:, 1, :], r_c[:, 1, :], r_c[:, 2, :], ALU.max))
                    step(V.tensor_tensor(gsum[:].rearrange("p j g -> p (j g)"), r_c[:, 0, :], r_c[:, 1, :], ALU.add))
                    other = gsum[:].unsqueeze(2).to_broadcast((P, TT, NGRP, NGRP))
                    this = gsum[:].unsqueeze(3).to_broadcast((P, TT, NGRP, NGRP))
                    step(V.tensor_tensor(cmp, other, this, ALU.is_gt))
                    step(V.tensor_tensor(cmp2, other, this, ALU.is_equal))
                    step(V.tensor_tensor(cmp2, cmp2,
                                         earlier[:].unsqueeze(1).to_broadcast((P, TT, NGRP, NGRP)), ALU.mult))
                    step(V.tensor_tensor(cmp, cmp, cmp2, ALU.add))
                    step(V.tensor_reduce(rank[:], cmp, AX.X, ALU.add))
                    step(V.tensor_scalar(rank[:], rank[:], float(TOPG), None, ALU.is_lt))
                    in_group = biased[:].rearrange("p j (g s) -> p (j g) s", s=GSZ)
                    step(V.tensor_tensor(in_group, in_group,
                                         rank[:].rearrange("p j g -> p (j g)").unsqueeze(2).to_broadcast(
                                             (P, TT * NGRP, GSZ)), ALU.mult))
                    for j in range(TT):
                        apart(dve)
                        step(V.max(top_v[:, j, :], biased[:, j, :]))
                    for j in range(TT):
                        apart(dve)
                        step(V.max_index(top_i[:, j, :], top_v[:, j, :], biased[:, j, :]))
                    step(V.tensor_copy(idx_f[:], top_i[:, :, 0:TOPK]))
                    idx = idx_f[:].rearrange("p j k -> p (j k)")
                    step(V.tensor_tensor(flat(one_hot), iota_f[:].unsqueeze(1).to_broadcast((P, TT * TOPK, NE)),
                                         idx.unsqueeze(2).to_broadcast((P, TT * TOPK, NE)), ALU.is_equal))
                    step(V.tensor_reduce(chosen[:], one_hot.rearrange("p j k e -> p j e k"), AX.X, ALU.add))
                    assert made[0] == R_CHOSEN
                    step(V.tensor_tensor(picked, one_hot, over_k(score[:]), ALU.mult))
                    step(V.tensor_reduce(wtmp[:], picked, AX.X, ALU.add))
                    step(V.tensor_reduce(wsum[:], wtmp[:], AX.X, ALU.add))
                    step(V.tensor_scalar(wsum[:], wsum[:], 1e-20, None, ALU.add))
                    step(V.reciprocal(wsum[:], wsum[:]))
                    step(V.tensor_tensor(wtmp[:], wtmp[:], wsum[:].unsqueeze(2).to_broadcast((P, TT, TOPK)),
                                         ALU.mult))
                    step(V.tensor_scalar(wtmp[:], wtmp[:], SCALE, None, ALU.mult))
                    assert made[0] == R_POS - 1, made[0]
                    return
                dve.wait_ge(t_pos, ch.at(1, 1))
                per_tile = misc_p[:, 0:TT * NE].rearrange("p (j e) -> p j e", e=NE)
                step(V.tensor_tensor(pos_all[:], per_tile, base[:].unsqueeze(1).to_broadcast((P, TT, NE)), ALU.add))
                step(V.tensor_tensor(base[:], misc_p[:, TT * NE:(TT + 1) * NE], base[:], ALU.add))
                step(V.tensor_tensor(picked, one_hot, over_k(pos_all[:]), ALU.mult))
                step(V.tensor_reduce(pos[:], picked, AX.X, ALU.add))
                step(V.scalar_tensor_tensor(slot_f[:], idx_f[:], float(CAP), pos[:], op0=ALU.mult, op1=ALU.add))
                step(V.tensor_scalar(valid[:], pos[:], float(CAP), None, ALU.is_lt))
                step(V.tensor_tensor(keep_w[:, bass.ds(ch.tile(0), TT), :], wtmp[:], valid[:], ALU.mult))
                step(V.tensor_scalar(pos[:], pos[:], float(CAP), FAR, ALU.is_ge, ALU.mult))
                step(V.tensor_tensor(slot_f[:], slot_f[:], pos[:], ALU.add))
                step(V.tensor_copy(keep_slot[:, bass.ds(ch.tile(0), TT), :], slot_f[:]))
                step(V.tensor_copy(slot_now[:], slot_f[:]))
                assert made[0] == R, made[0]

            def slot(now, ready, done):
                if now is None and ready is not None:
                    for j in range(TT):
                        prepare_stats(ready, j)
                        prepare_norm(ready, j)
                    for e in range(ET):
                        convolve(ready, e)
                    clamp_dt(ready, 0)
                    finish_dt(ready, 0)
                    dve.wait_ge(s_const, 48)
                    return
                if now is None:
                    gate_y(done, ET - 1)
                    for j in range(TT):
                        finish_stats(done, j)
                        finish_add(done, j)
                        finish_norm(done, j)
                    route(done, 0)
                    route(done, 1)
                    return
                for e in range(ET):
                    for g in range(NG):
                        scan(now, e, g)
                        if g > 0 and g - 1 not in POOL_GROUPS:
                            c_product(now, e, g - 1)
                        if g == 0 and e > 0:
                            c_product(now, e - 1, NG - 1)
                        keep_state(now, e, g)
                        if e == ET - 1 and g == NG - 1:
                            c_product(now, e, g)
                        if g == 1 and e > 0:
                            gate_y(now, e - 1)
                        if g == 1 and e == 0 and done is not None:
                            gate_y(done, ET - 1)
                        if ready is not None:
                            if e == 0 and 1 <= g <= TT:
                                prepare_norm(ready, g - 1)
                            if e == 0 and g < TT:
                                prepare_stats(ready, g)
                            if g == (6 if e == 0 else 2):
                                convolve(ready, e)
                            if e == ET - 1 and g == 6:
                                clamp_dt(ready, 0)
                            if e == ET - 1 and g == 7:
                                finish_dt(ready, 0)
                        if e < ET - 1 and g == 5:
                            clamp_dt(now, e + 1)
                        if e < ET - 1 and g == 7:
                            finish_dt(now, e + 1)
                        if done is not None:
                            if e < TT and g == 7:
                                finish_stats(done, e)
                            if 1 <= e <= TT and g == 1:
                                finish_add(done, e - 1)
                            if 1 <= e <= TT and g == 4:
                                finish_norm(done, e - 1)
                            if e == 5 and g == 0:
                                route(done, 0)
                            if e == 5 and g == 5:
                                route(done, 1)

            run_slots(dve, slot)


def experts(nc, keep_w, keep_slot, ident, minus_half, sup_t, sdown_t, wexp, out,
            xe_d, ye_d, x1_d, xft_d):
    with ExitStack() as ctx:
        def hold(stack, name, shape, dt=F32):
            return stack.enter_context(nc.sbuf_tensor(name, shape, dt))

        sup = hold(ctx, "sup", [P, KH, HS])
        sdown = hold(ctx, "sdown", [P, KHS, H])
        banks = [ctx.enter_context(nc.psum_tensor(f"bank{i}_p", [P, 512], F32)) for i in range(8)]
        s_shared = ctx.enter_context(nc.semaphore("shared_weights_loaded"))
        run_experts(nc, hold, banks, ident, sup, sdown, s_shared, sup_t, sdown_t, wexp, xe_d, ye_d)
        run_shared(nc, hold, banks, keep_w, keep_slot, minus_half, sup, sdown, s_shared, out,
                   ye_d, x1_d, xft_d)


class Expert:
    NW = 4

    def __init__(self, round_, i):
        self.round, self.i = round_, i

    def back(self, n):
        return Expert(self.round, self.i - n)

    def at(self, per, offset=0):
        return count(self.round * (self.NW * per) + (per * self.i + offset))

    def use(self, ring):
        return self.round * (self.NW // ring) + self.i // ring

    def there(self):
        return not isinstance(self.round, int) or 0 <= self.round * self.NW + self.i < NE


def run_experts(nc, hold, banks, ident, sup, sdown, s_shared, sup_t, sdown_t, wexp, xe_d, ye_d):
    NW = Expert.NW
    TS = CAP // P
    with ExitStack() as ctx:
        def sem(name):
            return ctx.enter_context(nc.semaphore(name))

        we = hold(ctx, "we", [P, NW, 2 * KH * HID])
        xe = hold(ctx, "xe", [P, NW, TS, H])
        xet = hold(ctx, "xet", [P, 2, KH, CAP])
        relu = hold(ctx, "relu", [P, 2, KHID * CAP])
        hid = hold(ctx, "hid", [P, 2, KHID, CAP])
        yo = hold(ctx, "yo", [P, 2, TS, H])
        up_w = we[:, :, 0:KH * HID].rearrange("p w (k m) -> p w k m", k=KH)
        down_w = we[:, :, KH * HID:].rearrange("p w (k d) -> p w k d", k=KHID)
        xt_p, up_p, down_p = banks[0:2], banks[2:4], banks[4:6]

        s_we = [sem(f"expert_weights{i}_loaded") for i in range(NW)]
        s_xe = [sem(f"expert_rows{i}_loaded") for i in range(NW)]
        s_ye = [sem(f"expert_out{i}_stored") for i in range(2)]
        t_x = sem("slots_transposed")
        a_x = sem("slots_copied")
        t_up = sem("up_done")
        a_relu = sem("relu_done")
        v_sq = sem("relu_squared")
        t_down = sem("down_done")
        v_y = sem("expert_out_copied")

        def rounds(eng, body, behind):
            for i in range(NW):
                body(Expert(0, i))
            with eng.Fori(1, NE // NW) as r:
                for i in range(NW):
                    body(Expert(r, i))
            for i in range(behind):
                body(Expert(NE // NW, i))

        def expert_rows(dram, x):
            return dram[bass.ds(x.at(CAP), CAP), :].rearrange("(s p) h -> p s h", p=P)

        block = ctx.enter_context(nc.Block())

        @block.sync
        def _(sp):
            def load(x):
                sp.wait_ge(t_down, x.at(TS, TS * (1 - NW)))
                sp.dma_start(we[:, x.i, :], wexp[bass.ds(x.at(1), 1), :, :].rearrange("a p c -> (a p) c")
                             ).then_inc(s_we[x.i], 16)
                sp.dma_start(xe[:, x.i], expert_rows(xe_d, x)).then_inc(s_xe[x.i], 16)

            rounds(sp, load, 0)
            sp.dma_start(sup[:], sup_t).then_inc(s_shared, 16)
            sp.dma_start(sdown[:], sdown_t).then_inc(s_shared, 16)
            sp.wait_ge(s_shared, 32)

        @block.gpsimd
        def _(pool):
            def store(x):
                pool.wait_ge(v_y, x.at(TS, TS))
                nc.gpsimd.dma_start(expert_rows(ye_d, x), yo[:, x.i % 2]).then_inc(s_ye[x.i % 2], 16)

            rounds(pool, store, 0)
            for s in s_ye:
                pool.wait_ge(s, 16 * NE // 2)

        @block.tensor
        def _(pe):
            def transpose_slots(x):
                pe.wait_ge(s_xe[x.i % NW], (x.use(NW) + 1) * 16)
                for s in range(TS):
                    pe.wait_ge(a_x, x.at(TS, s + 1 - TS))
                    for k in range(KH):
                        mm = nc.tensor.transpose(xt_p[s][:, k * P:(k + 1) * P],
                                                 xe[:, x.i % NW, s, k * P:(k + 1) * P], ident[:])
                    mm.then_inc(t_x, 1)

            def up(x):
                pe.wait_ge(a_x, x.at(TS, TS))
                pe.wait_ge(s_we[x.i % NW], (x.use(NW) + 1) * 16)
                pe.wait_ge(v_sq, x.at(1, -1))
                for m in range(KHID):
                    for k in range(KH):
                        mm = nc.tensor.matmul(up_p[x.i % 2][:, m * CAP:(m + 1) * CAP],
                                              up_w[:, x.i % NW, k, m * P:(m + 1) * P], xet[:, x.i % 2, k, :],
                                              start=(k == 0), stop=(k == KH - 1))
                mm.then_inc(t_up, 1)

            def down(x):
                pe.wait_ge(v_sq, x.at(1, 1))
                for s in range(TS):
                    pe.wait_ge(v_y, x.at(TS, s + 1 - TS))
                    for k in range(KHID):
                        mm = nc.tensor.matmul(down_p[s][:], hid[:, x.i % 2, k, s * P:(s + 1) * P],
                                              down_w[:, x.i % NW, k, :], start=(k == 0), stop=(k == KHID - 1))
                    mm.then_inc(t_down, 1)

            def turn(x):
                for stage, n in ((transpose_slots, 0), (up, 1), (down, 2)):
                    if x.back(n).there():
                        stage(x.back(n))

            rounds(pe, turn, 2)

        @block.scalar
        def _(act):
            def copy_slots(x):
                act.wait_ge(t_up, x.at(1, -1))
                for s in range(TS):
                    act.wait_ge(t_x, x.at(TS, s + 1))
                    nc.scalar.copy(xet[:, x.i % 2, :, s * P:(s + 1) * P],
                                   xt_p[s][:].rearrange("p (k t) -> p k t", k=KH)).then_inc(a_x, 1)

            def relus(x):
                act.wait_ge(t_up, x.at(1, 1))
                act.wait_ge(v_sq, x.at(1, -1))
                nc.scalar.activation(relu[:, x.i % 2, :], up_p[x.i % 2][:], ACT.Relu).then_inc(a_relu, 1)

            def turn(x):
                if x.there():
                    copy_slots(x)
                if x.back(1).there():
                    relus(x.back(1))

            rounds(act, turn, 1)

        @block.vector
        def _(dve):
            V = nc.vector

            def square(x):
                dve.wait_ge(a_relu, x.at(1, 1))
                dve.wait_ge(t_down, x.at(TS, -TS))
                V.tensor_tensor(hid[:, x.i % 2].rearrange("p k c -> p (k c)"), up_p[x.i % 2][:],
                                relu[:, x.i % 2, :], ALU.mult).then_inc(v_sq, 1)

            def copy_out(x):
                dve.wait_ge(s_ye[x.i % 2], x.use(2) * 16)
                for s in range(TS):
                    dve.wait_ge(t_down, x.at(TS, s + 1))
                    V.tensor_copy(yo[:, x.i % 2, s, :], down_p[s][:]).then_inc(v_y, 1)

            def turn(x):
                if x.back(1).there():
                    square(x.back(1))
                if x.back(2).there():
                    copy_out(x.back(2))

            rounds(dve, turn, 2)


def run_shared(nc, hold, banks, keep_w, keep_slot, minus_half, sup, sdown, s_shared, out,
               ye_d, x1_d, xft_d):
    with ExitStack() as ctx:
        def sem(name):
            return ctx.enter_context(nc.semaphore(name))

        xfc = hold(ctx, "xfc", [P, 2, TT, KH * P])
        relu = hold(ctx, "relu_s", [P, 2, CH])
        hsh = hold(ctx, "hsh", [P, 2, KHS, CH])
        rows = hold(ctx, "rows", [P, TT, TOPK, H])
        x1t = hold(ctx, "x1t", [P, TT, H])
        acc = hold(ctx, "acc_f", [P, TT, H])
        slots = hold(ctx, "slots", [P, TT, TOPK], I32)
        st = hold(ctx, "st_f", [P, 6])
        mv = hold(ctx, "mv_f", [P, 2, 2])
        rstd = hold(ctx, "rstd_f", [P, 2])
        up_p, down_p = banks[0:4], banks[4:8]

        s_xfc = [sem(f"xfc{i}_loaded") for i in range(2)]
        s_x1 = [sem(f"x1t{j}_loaded") for j in range(TT)]
        s_rows = [sem(f"rows{j}_gathered") for j in range(TT)]
        s_out = [sem(f"out{j}_stored") for j in range(TT)]
        t_up = sem("shared_up")
        a_relu = sem("shared_relu")
        v_sq = sem("shared_squared")
        t_down = sem("shared_down")
        g_slots = sem("slots_copied_f")
        v_sum = sem("sum_steps")
        g_r = sem("final_rstd")
        v_fin = sem("final_steps")

        x1_tiles = x1_d.rearrange("(i p) h -> i p h", p=P)
        out_tiles = out.rearrange("(i p) h -> i p h", p=P)

        def chunks(eng, slot):
            slot(Chunk(0, 0), None)
            with eng.Fori(0, NPAIR - 1) as r:
                for ready in (Chunk(r, 1), Chunk(r + 1, 0)):
                    slot(ready, ready.prev())
            slot(Chunk(NPAIR - 1, 1), Chunk(NPAIR - 1, 0))
            slot(None, Chunk(NPAIR - 1, 1))

        block = ctx.enter_context(nc.Block())

        @block.sync
        def _(sp):
            def load_xfc(ch):
                sp.wait_ge(t_up, ch.at(KHS, -KHS))
                sp.dma_start(xfc[:, ch.half], xft_d[bass.ds(ch.tile(0), TT), :, :].rearrange("i p c -> p i c")
                             ).then_inc(s_xfc[ch.half], 16)

            def load_x1(ch, j):
                sp.wait_ge(v_fin, ch.at(2 * TT, 2 * (j + 1 - TT)))
                sp.dma_start(x1t[:, j], x1_tiles[bass.ds(ch.tile(j), 1), :, :].rearrange("a p h -> (a p) h")
                             ).then_inc(s_x1[j], 16)

            def store(ch, j):
                sp.wait_ge(v_fin, ch.at(2 * TT, 2 * j + 2))
                sp.dma_start(out_tiles[bass.ds(ch.tile(j), 1), :, :].rearrange("a p h -> (a p) h"),
                             acc[:, j]).then_inc(s_out[j], 16)

            def slot(ready, done):
                if done is None:
                    load_xfc(ready)
                if ready is not None and not (isinstance(ready.pair, int) and ready.at(1) == NCHUNK - 1):
                    load_xfc(ready.next())
                for j in range(TT):
                    if done is not None:
                        store(done, j)
                    if ready is not None:
                        load_x1(ready, j)

            chunks(sp, slot)
            for s in s_out:
                sp.wait_ge(s, 16 * NCHUNK)

        @block.gpsimd
        def _(pool):
            def gather(ch, j):
                nc.gpsimd.tensor_copy(slots[:, j, :], keep_slot[:, bass.ds(ch.tile(j), 1), :].rearrange(
                    "p a k -> p (a k)")).then_inc(g_slots, 1)
                pool.wait_ge(g_slots, ch.tile(j + 1))
                pool.wait_ge(v_sum, ch.at(6 * TT, 6 * j + 4))
                apart(pool)
                for k in range(TOPK):
                    nc.gpsimd.indirect_dma_start(
                        rows[:, j, k, :], None, ye_d,
                        bass.IndirectOffsetOnAxis(ap=slots[:, j, k:k + 1].bitcast(U32), axis=0),
                        bounds_check=NE * CAP - 1, oob_is_err=False).then_inc(s_rows[j], 16)

            def final_rstd(ch, j):
                b = j % 2
                pool.wait_ge(v_sum, ch.at(6 * TT, 6 * (j + TT) + 6))
                apart(pool)
                nc.gpsimd.tensor_scalar(rstd[:, b:b + 1], mv[:, b, 1:2], EPS, None, ALU.add).then_inc(g_r, 1)
                pool.wait_ge(g_r, ch.at(2 * TT, 2 * j + 1))
                nc.gpsimd.tensor_tensor(rstd[:, b:b + 1], rstd[:, b:b + 1], minus_half[:], ALU.pow
                                        ).then_inc(g_r, 1)

            def slot(ready, done):
                for j in range(TT):
                    if done is not None:
                        final_rstd(done, j)
                    if ready is not None:
                        gather(ready, j)

            chunks(pool, slot)

        @block.tensor
        def _(pe):
            pe.wait_ge(s_shared, 32)

            def up(ch, m):
                if m == 0:
                    pe.wait_ge(s_xfc[ch.half], ch.pair * 16 + 16)
                pe.wait_ge(v_sq, ch.at(KHS, m - 3))
                for k in range(KH):
                    mm = nc.tensor.matmul(up_p[m % 4][:].rearrange("p (i t) -> p i t", i=TT),
                                          sup[:, k, m * P:(m + 1) * P],
                                          xfc[:, ch.half, :, k * P:(k + 1) * P],
                                          start=(k == 0), stop=(k == KH - 1))
                mm.then_inc(t_up, 1)

            def down(ch, j):
                if j == 0:
                    pe.wait_ge(v_sq, ch.at(KHS, KHS))
                pe.wait_ge(v_sum, ch.at(6 * TT, 6 * j + 1))
                for m in range(KHS):
                    mm = nc.tensor.matmul(down_p[j][:], hsh[:, ch.half, m, j * P:(j + 1) * P], sdown[:, m, :],
                                          start=(m == 0), stop=(m == KHS - 1))
                mm.then_inc(t_down, 1)

            def slot(ready, done):
                for j in range(TT):
                    if ready is not None:
                        up(ready, 2 * j)
                        up(ready, 2 * j + 1)
                    if done is not None:
                        down(done, j)

            chunks(pe, slot)

        @block.scalar
        def _(act):
            def slot(ready, done):
                if ready is not None:
                    for m in range(KHS):
                        act.wait_ge(t_up, ready.at(KHS, m + 1))
                        act.wait_ge(v_sq, ready.at(KHS, m - 1))
                        nc.scalar.activation(relu[:, m % 2, :], up_p[m % 4][:], ACT.Relu).then_inc(a_relu, 1)

            chunks(act, slot)

        @block.vector
        def _(dve):
            V = nc.vector
            V.memset(rows[:], 0.0).then_inc(v_sum, 6 * TT)
            dve.wait_ge(v_sum, 6 * TT)

            def square(ch, m):
                dve.wait_ge(a_relu, ch.at(KHS, m + 1))
                if m == 0:
                    dve.wait_ge(t_down, ch.at(TT, -TT))
                V.tensor_tensor(hsh[:, ch.half, m, :], up_p[m % 4][:], relu[:, m % 2, :], ALU.mult
                                ).then_inc(v_sq, 1)

            def add_up(ch, j):
                made = [0]

                def step(ins):
                    made[0] += 1
                    ins.then_inc(v_sum, 1)
                    dve.wait_ge(v_sum, ch.at(6 * TT, 6 * (j + TT) + made[0]))

                dve.wait_ge(t_down, ch.tile(j + 1))
                dve.wait_ge(s_rows[j], ch.at(16 * TOPK, 16 * TOPK))
                dve.wait_ge(s_out[j], ch.at(16, 0))
                for k in range(TOPK):
                    weight = keep_w[:, bass.ds(ch.tile(j), 1), k:k + 1].rearrange("p a k -> p (a k)")
                    step(V.scalar_tensor_tensor(acc[:, j, :], rows[:, j, k, :], weight,
                                                acc[:, j, :] if k else down_p[j][:], op0=ALU.mult, op1=ALU.add))
                step(V.bn_stats(st[:], acc[:, j, :]))
                apart(dve)
                step(V.bn_aggr(mv[:, j % 2, :], st[:]))

            def finish(ch, j):
                dve.wait_ge(g_r, ch.at(2 * TT, 2 * j + 2))
                V.tensor_scalar(acc[:, j, :], acc[:, j, :], mv[:, j % 2, 0:1], rstd[:, j % 2:j % 2 + 1],
                                ALU.subtract, ALU.mult).then_inc(v_fin, 1)
                dve.wait_ge(v_fin, ch.at(2 * TT, 2 * j + 1))
                dve.wait_ge(s_x1[j], ch.at(16, 16))
                V.tensor_tensor(acc[:, j, :], acc[:, j, :], x1t[:, j, :], ALU.add).then_inc(v_fin, 1)

            def slot(ready, done):
                for j in range(TT):
                    if ready is not None:
                        square(ready, 2 * j)
                        square(ready, 2 * j + 1)
                    if done is not None:
                        add_up(done, j)
                        if j:
                            finish(done, j - 1)
                if done is not None:
                    finish(done, TT - 1)

            chunks(dve, slot)


def kernel(**inputs):
    import numpy as np
    import concourse.bacc as bacc
    from concourse.bass_utils import run_bass_kernel_spmd

    a = {k: np.ascontiguousarray(v) for k, v in inputs.items()}
    w_in = a["L0_attn_W_in"].reshape(KH, P, 2, ET, P)
    w_in = w_in.transpose(3, 1, 2, 0, 4).reshape(ET, P, 2, KH * P)
    w_x = a["L0_attn_W_x"].reshape(ET, P, TR + 2 * N)
    w_dt = a["L0_attn_W_dt"].reshape(TR, ET, P).transpose(1, 0, 2)

    def channels(v, width=1):
        return v.reshape(ET, P, width).transpose(1, 0, 2)

    def rows(w, k):
        return w.reshape(k, P, -1).transpose(1, 0, 2)

    up = a["L0_ffn_up_w"].transpose(0, 2, 1).reshape(NE, KH, P, HID).transpose(0, 2, 1, 3)
    down = a["L0_ffn_down_w"].transpose(0, 2, 1).reshape(NE, KHID, P, H).transpose(0, 2, 1, 3)
    arrays = {
        "x": a["L0_attn_input_states"].reshape(T, H),
        "wpack": np.concatenate([w_in[:, :, 0], w_x, w_dt], axis=2),
        "wgate": w_in[:, :, 1],
        "params": np.concatenate([
            channels(a["L0_attn_conv_kernel"], TAPS), channels(a["L0_attn_conv_bias"]),
            channels(a["L0_attn_b_dt"]), channels(a["L0_attn_D"]), channels(a["L0_attn_A_log"], N)], axis=2),
        "w_out": rows(a["L0_attn_W_out"], ET),
        "gate_t": rows(a["L0_ffn_gate_w"].T, KH),
        "bias_bc": np.broadcast_to(a["L0_ffn_bias_corr"][None, :], (P, NE)),
        "sup_t": rows(a["L0_ffn_shared_up_w"].T, KH),
        "sdown_t": rows(a["L0_ffn_shared_down_w"].T, KHS),
        "wexp": np.concatenate([up.reshape(NE, P, -1), down.reshape(NE, P, -1)], axis=2),
    }
    nc = bacc.Bacc("TRN2", target_bir_lowering=False, num_devices=1, dynamic_dma_scratch_size=8192)
    arrays = {f"in_{k}": np.ascontiguousarray(v) for k, v in arrays.items()}
    args = [nc.dram_tensor(k, v.shape, mybir.dt.from_np(v.dtype), kind="ExternalInput").ap()
            for k, v in arrays.items()]
    args.append(nc.dram_tensor("out_dram", (T, H), F32, kind="ExternalOutput").ap())
    for name, shape in (("xe_scratch", (NE * CAP, H)), ("ye_scratch", (NE * CAP, H)),
                        ("x1_scratch", (T, H)), ("xft_scratch", (NTILE, P, KH * P))):
        args.append(nc.dram_tensor(name, shape, F32, kind="Internal").ap())
    sandwich(nc, *args)
    r = run_bass_kernel_spmd(nc, [arrays], core_ids=[0])
    return r.results[0]["out_dram"].reshape(BATCH, SEQ, H)
```

```python
from contextlib import ExitStack

import concourse.bass as bass
from concourse import mybir

ALU = mybir.AluOpType
ACT = mybir.ActivationFunctionType
F32 = mybir.dt.float32
I32 = mybir.dt.int32
U32 = mybir.dt.uint32
AX = mybir.AxisListType

P = 128
EPS = 1e-5
EXP_LN_SET = "natural_log_exp_and_others"

T, H, E, N, TR, TAPS, BATCH = 4096, 512, 1024, 16, 128, 4, 4
SEQ = T // BATCH
CH = 512
NCHUNK = T // CH
NPAIR = NCHUNK // 2
ET = E // P
KH = H // P
TT = CH // P
GN = 2
NG = N // GN
RING = 4
POOL_GROUPS = [()] + [(1, 4)] * 4 + [(1, 3, 5), (1,), ()]

PROJECT = [((0, 5), (0, 6)), ((1, 1), (1, 2))] + [((e - 1, 6), (e - 1, 7)) for e in range(2, 8)]
TAP = [(0, 7), (1, 4)] + [(e, 3) for e in range(2, 7)] + [(7, 2)]
CONV = [(1, 0), (1, 4)] + [(e, 4) for e in range(2, 7)] + [(7, 1)]
SILU = [(1, 3), (1, 7)] + [(e, 6) for e in range(2, 7)] + [(7, 3)]
TIMES_WX = [(1, 4), (2, 1)] + [(e + 1, 1) for e in range(2, 7)] + [(7, 4)]
GATE = [((e, 2 + 2 * h), (e, 3 + 2 * h)) for e in range(4, 7) for h in range(2)] + [
    ((7, 1), (7, 2)), ((7, 5), (7, 6))]
SILU_GATE = [(4, 6), (5, 2), (5, 6), (6, 2), (6, 6), (7, 2), (7, 4), (8, 2)]
ROUTE = [(5, 3), (5, 4), (5, 5), (5, 6), (6, 0), (6, 1), (6, 2)]

NE, NGRP, TOPG, TOPK, HID, HS, CAP, SCALE = 32, 8, 4, 4, 256, 1024, 256, 2.5
GSZ = NE // NGRP
KHID, KHS = HID // P, HS // P
NTILE = T // P
FAR = 65536.0

WIN, WX = 0, KH * P
WPACK = WX + TR + 2 * N
NPAR = TAPS + 3 + N


def apart(eng):
    eng.nop(nofuse=True)


def count(value):
    return max(value, 0) if isinstance(value, int) else value


class Chunk:

    def __init__(self, pair, half):
        self.pair, self.half = pair, half

    def next(self):
        return Chunk(self.pair, 1) if self.half == 0 else Chunk(self.pair + 1, 0)

    def prev(self):
        return Chunk(self.pair, 0) if self.half == 1 else Chunk(self.pair + (-1), 1)

    def at(self, per, offset=0):
        return count(self.pair * (2 * per) + (per * self.half + offset))

    def unit(self, e):
        return self.at(ET, e)

    def group(self, e, g):
        return self.at(ET * NG, e * NG + g)

    def tile(self, j):
        return self.at(TT, j)


def run_slots(eng, slot):
    slot(None, Chunk(0, 0), None)
    slot(Chunk(0, 0), Chunk(0, 1), None)
    with eng.Fori(0, NPAIR - 1) as r:
        for now in (Chunk(r, 1), Chunk(r + 1, 0)):
            slot(now, now.next(), now.prev())
    last = Chunk(NPAIR - 1, 1)
    slot(last, None, last.prev())
    slot(None, None, last)


def copies7(ch, k, preparing):
    per, known = 3 * TT, isinstance(ch.pair, int)
    if preparing:
        if known and ch.at(1) < 2:
            return ch.at(1) * TT + k
        return ch.at(per, 2 * TT - 2 * per + k)
    if known and ch.at(1) >= NCHUNK - 2:
        return 2 * TT + per * (NCHUNK - 2) + 2 * TT * (ch.at(1) - (NCHUNK - 2)) + k
    return ch.at(per, 3 * TT + k)


def sandwich(nc, x, wpack, wgate, params, w_dt, w_out, gate_t, bias_bc, sup_t, sdown_t, wexp, out,
             xe_d, ye_d, x1_d, xft_d, bc_d):
    outer = ExitStack()
    with outer:
        keep_w = outer.enter_context(nc.sbuf_tensor("route_w", [P, NTILE, TOPK], F32))
        keep_slot = outer.enter_context(nc.sbuf_tensor("route_slot", [P, NTILE, TOPK], I32))
        ident = outer.enter_context(nc.sbuf_tensor("ident", [P, P], F32))
        minus_half = outer.enter_context(nc.sbuf_tensor("minus_half", [P, 1], F32))
        mixer(nc, keep_w, keep_slot, ident, minus_half, x, wpack, wgate, params, w_dt, w_out, gate_t, bias_bc,
              xe_d, x1_d, xft_d, bc_d)
        experts(nc, keep_w, keep_slot, ident, minus_half, sup_t, sdown_t, wexp, out,
                xe_d, ye_d, x1_d, xft_d)


def mixer(nc, keep_w, keep_slot, ident, minus_half, x, wpack, wgate, params, w_dt, w_out, gate_t, bias_bc,
          xe_d, x1_d, xft_d, bc_d):
    with ExitStack() as ctx:
        def sb(name, shape, dt=F32):
            return ctx.enter_context(nc.sbuf_tensor(name, shape, dt))

        def sem(name):
            return ctx.enter_context(nc.semaphore(name))

        b_bc = sb("b_bc", [P, N, CH])
        c_bc = sb("c_bc", [P, N, CH])
        hs = sb("hs", [P, ET, CH])
        gy = sb("gy", [P, 2, ET, CH])
        xnt = sb("xnt", [P, KH, CH])
        dt_t = sb("dt_t", [P, CH])
        wout_sb = sb("wout_sb", [P, ET, H])
        wp = sb("wp", [P, 2, WPACK])
        wdt_sb = sb("wdt_sb", [P, ET, P])
        wg = sb("wg", [P, 2, KH * P])
        par = sb("par", [P, ET, NPAR])
        a_neg = par[:, :, NPAR - N:NPAR]
        a_buf = sb("a_buf", [P, RING, GN, CH])
        h_buf = sb("h_buf", [P, RING, GN, CH])
        dts = sb("dts", [P, 2, CH])
        dtu = sb("dtu", [P, 2, CH])
        du = sb("du", [P, 2, CH])
        tail = sb("tail", [P, ET, TAPS - 1])
        state = sb("state", [P, ET, N])
        x_in = sb("x_in", [P, 2, H])
        x1 = sb("x1", [P, H])
        xf = sb("xf", [P, TT, H])
        xft = sb("xft", [P, KH * P])
        gate_sb = sb("gate_sb", [P, KH, NE])
        bias_sb = sb("bias_sb", [P, NE])
        before = sb("before", [P, P])
        ones = sb("ones", [P, P])
        st = sb("st", [P, 3, 6])
        mv = sb("mv", [P, 3, 2])
        rstd = sb("rstd", [P, 3])
        score = sb("score", [P, TT, NE])
        biased = sb("biased", [P, TT, NE])
        bc_t = xft[0:2 * N, :]
        cmp = xft[:, 0:TT * NGRP * NGRP].rearrange("p (j g h) -> p j g h", j=TT, g=NGRP)
        cmp2 = xft[:, TT * NGRP * NGRP:].rearrange("p (j g h) -> p j g h", j=TT, g=NGRP)
        earlier = sb("earlier", [P, NGRP, NGRP])
        rank = sb("rank", [P, TT, NGRP])
        top_v = sb("top_v", [P, TT, 8])
        top_i = sb("top_i", [P, TT, 8], U32)
        idx_f = sb("idx_f", [P, TT, TOPK])
        q = TT * NGRP
        r_a = x_in[:, 0, 0:2 * q].rearrange("p (q two) -> p q two", two=2)
        r_b = x_in[:, 0, 2 * q:4 * q].rearrange("p (q two) -> p q two", two=2)
        r_c = x_in[:, 0, 4 * q:7 * q].rearrange("p (c q) -> p c q", c=3)
        gsum = x_in[:, 0, 7 * q:8 * q].rearrange("p (j g) -> p j g", j=TT)
        one_hot = x_in[:, 0, :].rearrange("p (j k e) -> p j k e", j=TT, k=TOPK)
        picked = x_in[:, 1, :].rearrange("p (j k e) -> p j k e", j=TT, k=TOPK)
        chosen = sb("chosen", [P, TT, NE])
        wtmp = sb("wtmp", [P, TT, TOPK])
        valid = sb("valid", [P, TT, TOPK])
        slot_now = sb("slot_now", [P, TT, TOPK], I32)
        iota_i = sb("iota_i", [P, NE], I32)
        iota_f = sb("iota_f", [P, NE])
        pos_all = biased
        base = sb("base", [P, NE])
        pos = sb("pos", [P, TT, TOPK])
        slot_f = sb("slot_f", [P, TT, TOPK])
        wsum = sb("wsum", [P, TT])

        def bank(name):
            return ctx.enter_context(nc.psum_tensor(name, [P, 512], F32))

        hid_p, gate_p, dtacc_p, bcacc_p, dts_p = (bank(f"{n}_p") for n in ("hid", "gt", "dta", "bca", "dts"))
        y_p = [bank("y0_p"), bank("y1_p")]
        misc_p = bank("misc_p")

        s_par = sem("params_loaded")
        s_wdt = sem("w_dt_loaded")
        s_const = sem("const_loaded")
        s_w = [sem("wpack0_loaded"), sem("wpack1_loaded")]
        s_wg = [sem("wgate0_loaded"), sem("wgate1_loaded")]
        s_x = [sem("x_in0_loaded"), sem("x_in1_loaded")]
        s_x1 = sem("x1_loaded")
        s_x1_out = sem("x1_stored")
        s_xft_out = sem("xft_stored")
        s_zero = sem("slots_zeroed")
        s_scat = sem("rows_scattered")
        g_setup = sem("pool_setup")
        v_setup = sem("dve_setup")
        a_setup = sem("act_setup")
        v_ln1 = sem("ln1_steps")
        g_ln1 = sem("ln1_rstd")
        t_ln1 = sem("ln1_transposed")
        t_hid = sem("hidden_projected")
        t_gp = sem("gate_projected")
        a_tap = sem("tap_done")
        v_conv = sem("conv_steps")
        a_hs = sem("hidden_silu")
        a_gs = sem("gate_silu")
        t_wx = sem("wx_done")
        a_dtbc = sem("dt_bc_copied")
        s_bc_out = sem("bc_stored")
        s_b = [sem(f"b{g}_spread") for g in range(NG)]
        s_c = [sem(f"c{g}_spread") for g in range(NG)]
        t_dts = sem("dt_projected")
        v_clamp = sem("dt_clamped")
        a_sp = sem("softplus_steps")
        v_dts = sem("dts_ready")
        v_dtu = sem("dtu_ready")
        a_exp = sem("decay_ready")
        g_dbu = sem("input_ready")
        v_scan = sem("scanned")
        v_keep = sem("states_kept")
        v_cp = sem("c_product_dve")
        g_cp = sem("c_product_pool")
        a_skip = sem("skip_term_ready")
        t_sum = sem("states_summed")
        v_sum_y = sem("skip_term_added")
        v_y = sem("y_ready")
        t_out = sem("w_out_done")
        v_c = sem("finish_steps")
        g_c = sem("finish_rstd")
        t_xft = sem("xf_transposed")
        t_gate = sem("gate_done")
        v_r = sem("route_steps")
        t_pos = sem("pos_counted")
        a_c7 = sem("bank7_copied")

        def c_count(ch, e, g):
            in_chunk = sum(len(q) for q in POOL_GROUPS)
            mine = sum(len(q) for q in POOL_GROUPS[:e]) + sum(q <= g for q in POOL_GROUPS[e])
            return ch.at(ET * NG - in_chunk, e * NG + g + 1 - mine), ch.at(in_chunk, mine)

        def wait_c_product(eng, ch, e, g):
            dve, pool = c_count(ch, e, g)
            if g in POOL_GROUPS[e]:
                eng.wait_ge(g_cp, pool)
            else:
                eng.wait_ge(v_cp, dve)

        def first(ch):
            return isinstance(ch.pair, int) and ch.at(1) == 0

        def last(ch):
            return isinstance(ch.pair, int) and ch.at(1) == NCHUNK - 1

        def out_bank(ch, j):
            return (gate_p, hid_p, dtacc_p, bcacc_p)[j] if last(ch) else gate_p

        def wait_kept(eng, ch, e, g):
            if ch.half == 0:
                eng.wait_ge(v_keep, ch.pair * (ET * NG) + (e * NG + g + 1))

        def conv_count(ch, e, done):
            per = (2 * (TAPS - 1)) if ch.half else (TAPS - 1)
            return ch.pair * (ET * 3 * (TAPS - 1)) + (ch.half * ET * (TAPS - 1) + e * per + done)

        def conv_all(ch, e):
            return conv_count(ch, e, 2 * (TAPS - 1) if ch.half else TAPS - 1)

        x_tiles = x.rearrange("(i p) h -> i p h", p=P)
        x1_tiles = x1_d.rearrange("(i p) h -> i p h", p=P)
        R_PART = (0, 10, 17, 25, 28, 35, 40, 46)
        R, R_CHOSEN = R_PART[-1], R_PART[4]

        block = ctx.enter_context(nc.Block())

        @block.sync
        def _(sp):
            def load_pack(v, e, freed_by, count):
                sp.wait_ge(freed_by, count)
                sp.dma_start(wp[:, e % 2, :], wpack[e]).then_inc(s_w[e % 2], 16)

            def load_gate(ch, e):
                sp.wait_ge(t_gp, ch.unit(e - 1))
                sp.dma_start(wg[:, e % 2, :], wgate[e]).then_inc(s_wg[e % 2], 16)

            def tile_of(dram, i):
                return dram[bass.ds(i, 1), :, :].rearrange("a p h -> (a p) h")

            def load_x(ch, j):
                sp.wait_ge(t_ln1, ch.tile(j - 1))
                apart(sp)
                sp.wait_ge(v_r, ch.at(R, -2 * R))
                apart(sp)
                sp.dma_start(x_in[:, j % 2, :], tile_of(x_tiles, ch.tile(j))).then_inc(s_x[j % 2], 16)

            def store_bc(ch):
                sp.wait_ge(a_dtbc, ch.at(2, 2))
                sp.dma_start(bc_d[bass.ds(ch.at(1), 1), :, :].rearrange("a n t -> (a n) t"), bc_t
                             ).then_inc(s_bc_out, 16)

            def spread(ch, g):
                sp.wait_ge(s_bc_out, ch.at(16, 16))
                for wide, first_row, done in ((b_bc, 0, s_b), (c_bc, N, s_c)):
                    rows = bc_d[bass.ds(ch.at(1), 1), first_row + g * GN:first_row + (g + 1) * GN, :]
                    if not first(ch):
                        apart(sp)
                        if wide is b_bc:
                            sp.wait_ge(g_dbu, ch.at(ET * NG, g + 1 - NG))
                        else:
                            wait_c_product(sp, ch.prev(), ET - 1, g)
                    apart(sp)
                    sp.dma_start(wide[:, g * GN:(g + 1) * GN, :], rows.to_broadcast((P, GN, CH))
                                 ).then_inc(done[g], 16)

            def load_x1(ch, j):
                sp.wait_ge(s_x1_out, ch.at(16 * TT, 16 * j))
                apart(sp)
                sp.wait_ge(v_c, ch.at(7 * TT, 7 * j))
                apart(sp)
                sp.dma_start(x1[:], tile_of(x_tiles, ch.tile(j))).then_inc(s_x1, 16)

            def store_x1(ch, j):
                sp.wait_ge(v_c, ch.at(7 * TT, 7 * j + 4))
                sp.dma_start(tile_of(x1_tiles, ch.tile(j)), x1[:]).then_inc(s_x1_out, 16)

            def store_xft(ch, j):
                sp.wait_ge(a_c7, copies7(ch, 2 * j, False) + 1)
                sp.dma_start(xft_d[bass.ds(ch.tile(j), 1), :, :].rearrange("a p c -> (a p) c"),
                             xft[:]).then_inc(s_xft_out, 16)

            sp.dma_start(par[:], params).then_inc(s_par, 16)
            sp.dma_start(wdt_sb[:], w_dt).then_inc(s_wdt, 16)

            def slot(now, ready, done):
                if now is not None:
                    store_bc(now)
                for j in range(TT):
                    if ready is not None:
                        load_x(ready, j)
                    if now is not None:
                        for g in (range(0), range(NG // 2), range(NG // 2, NG * 3 // 4),
                                  range(NG * 3 // 4, NG))[j]:
                            spread(now, g)
                    elif ready is not None and j == 1:
                        for e in range(2):
                            load_pack(e, e, t_wx, 0)
                        sp.dma_start(wout_sb[:], w_out).then_inc(s_const, 16)
                        sp.dma_start(gate_sb[:], gate_t).then_inc(s_const, 16)
                        sp.dma_start(bias_sb[:], bias_bc).then_inc(s_const, 16)
                for e in range(ET):
                    if done is not None and 2 <= e <= TT + 1:
                        store_xft(done, e - 2)
                    if done is not None and 1 <= e <= TT:
                        store_x1(done, e - 1)
                    if done is not None and e < TT:
                        load_x1(done, e)
                    if now is None and ready is not None:
                        for q in (0, 1) if e == 0 else range(e + 1, min(e + 2, ET)):
                            load_gate(ready, q)
                        load_pack(e + 2, (e + 2) % ET, t_wx, e + 1)
                    elif ready is not None:
                        for q in (2 * e + 2 - ET, 2 * e + 3 - ET):
                            if 0 <= q < ET:
                                load_gate(ready, q)
                        load_pack(now.unit(ET + e + 2), (e + 2) % ET, t_wx, now.unit(ET + e + 1))

            run_slots(sp, slot)
            for s in s_w:
                sp.wait_ge(s, 16 * (ET * NCHUNK + 2) // 2)
            sp.wait_ge(s_x1_out, 16 * NTILE)
            sp.wait_ge(s_xft_out, 16 * NTILE)
            sp.wait_ge(s_scat, 16 * NTILE * TOPK)

        @block.gpsimd
        def _(pool):
            setup = [0]

            def step(ins):
                setup[0] += 1
                ins.then_inc(g_setup, 1)

            step(nc.gpsimd.memset(ident[:], 0.0))
            step(nc.gpsimd.memset(xf[:, 0, :], 0.0))
            step(nc.gpsimd.memset(ones[:], 1.0))
            step(nc.gpsimd.memset(before[:], 1.0))
            step(nc.gpsimd.memset(earlier[:], 1.0))
            step(nc.gpsimd.memset(minus_half[:], -0.5))
            step(nc.gpsimd.iota(iota_i[:], pattern=[[1, NE]], base=0, channel_multiplier=0))
            pool.wait_ge(g_setup, 7)
            step(nc.gpsimd.affine_select(out=ident[:], in_=ident[:], compare_op=ALU.not_equal, fill=1.0,
                                         base=0, pattern=[[-1, P]], channel_multiplier=1))
            step(nc.gpsimd.affine_select(out=before[:], in_=before[:], compare_op=ALU.is_gt, fill=0.0,
                                         base=0, pattern=[[1, P]], channel_multiplier=-1))
            step(nc.gpsimd.affine_select(out=earlier[:], in_=earlier[:], compare_op=ALU.is_gt, fill=0.0,
                                         base=0, pattern=[[1, NGRP], [-1, NGRP]], channel_multiplier=0))
            step(nc.gpsimd.tensor_copy(iota_f[:], iota_i[:]))
            pool.wait_ge(g_setup, 11)
            pool.wait_ge(s_par, 16)

            def input_term(ch, e, g):
                u, q = ch.unit(e), ch.group(e, g)
                if g == 0:
                    pool.wait_ge(v_dtu, ch.unit(e + 1))
                if e == 0:
                    pool.wait_ge(s_b[g], ch.at(16, 16))
                pool.wait_ge(t_sum, ch.group(e, g + 1 - RING))
                nc.gpsimd.tensor_tensor(
                    h_buf[:, g % RING], dtu[:, e % 2, :].unsqueeze(1).to_broadcast((P, GN, CH)),
                    b_bc[:, g * GN:(g + 1) * GN, :], ALU.mult).then_inc(g_dbu, 1)

            def c_product(ch, e, g):
                pool.wait_ge(v_scan, ch.at(ET * N, e * N + (g + 1) * GN))
                wait_kept(pool, ch, e, g)
                if e == 0:
                    pool.wait_ge(s_c[g], ch.at(16, 16))
                nc.gpsimd.tensor_tensor(h_buf[:, g % RING], h_buf[:, g % RING],
                                        c_bc[:, g * GN:(g + 1) * GN, :], ALU.mult).then_inc(g_cp, 1)

            def rstd_of(k, sem_in, count_in, sem_out, count_out):
                pool.wait_ge(sem_in, count_in)
                apart(pool)
                nc.gpsimd.tensor_scalar(rstd[:, k:k + 1], mv[:, k, 1:2], EPS, None, ALU.add).then_inc(sem_out, 1)
                pool.wait_ge(sem_out, count_out)
                nc.gpsimd.tensor_tensor(rstd[:, k:k + 1], rstd[:, k:k + 1], minus_half[:], ALU.pow
                                        ).then_inc(sem_out, 1)

            def prepare_norm(ch, j):
                rstd_of(0, v_ln1, ch.at(3 * TT, 3 * j + 2), g_ln1, ch.at(2 * TT, 2 * j + 1))

            def finish_norm(ch, j, k):
                rstd_of(1 + k, v_c, ch.at(7 * TT, 7 * j + 2 + 4 * k), g_c, ch.at(4 * TT, 4 * j + 2 * k + 1))

            def scatter(ch, m):
                j, k = m // TOPK, m % TOPK
                if m == 0:
                    pool.wait_ge(v_r, ch.at(R, R))
                    pool.wait_ge(s_zero, 16 * ET)
                apart(pool)
                nc.gpsimd.indirect_dma_start(
                    xe_d, bass.IndirectOffsetOnAxis(ap=slot_now[:, j, k:k + 1].bitcast(U32), axis=0),
                    xf[:, j, :], None, bounds_check=NE * CAP - 1, oob_is_err=False).then_inc(s_scat, 16)

            def slot(now, ready, done):
                if now is None:
                    if ready is not None:
                        for j in range(TT):
                            prepare_norm(ready, j)
                    if done is not None:
                        for j in range(TT):
                            finish_norm(done, j, 0)
                            finish_norm(done, j, 1)
                        for m in range(TT * TOPK):
                            scatter(done, m)
                    return
                for e in range(ET):
                    for g in range(NG):
                        if g >= 2 and g - 2 in POOL_GROUPS[e]:
                            c_product(now, e, g - 2)
                        input_term(now, e, g)
                        if ready is not None and e == 0 and 1 <= g <= TT:
                            prepare_norm(ready, g - 1)
                        if done is not None:
                            if 1 <= e <= TT and g == 1:
                                finish_norm(done, e - 1, 0)
                            if 1 <= e <= TT and g == 5:
                                finish_norm(done, e - 1, 1)
                            if e == 6 and g >= 4:
                                scatter(done, 2 * (g - 4))
                                scatter(done, 2 * (g - 4) + 1)
                            if e == 7:
                                scatter(done, NG + g)

            run_slots(pool, slot)

        @block.scalar
        def _(act):
            act.wait_ge(g_setup, 2)
            zero_rows = xe_d.rearrange("(u p r) h -> u p r h", u=ET, p=P)

            def zero_slots(u):
                act.dma_start(zero_rows[u], xf[:, 0, :].unsqueeze(1).to_broadcast((P, NE * CAP // P // ET, H))
                              ).then_inc(s_zero, 16)

            nc.scalar.preload_act_table_set(EXP_LN_SET)
            act.wait_ge(s_par, 16)
            nc.scalar.activation(a_neg, a_neg, ACT.Exp).then_inc(a_setup, 1)
            act.wait_ge(a_setup, 1)
            nc.scalar.mul(a_neg, a_neg, -1.0).then_inc(a_setup, 1)
            act.wait_ge(a_setup, 2)

            def xnt_copy(ch, j):
                act.wait_ge(t_ln1, ch.tile(j + 1))
                if j == 0:
                    act.wait_ge(t_hid, ch.unit(0))
                    act.wait_ge(t_gp, ch.unit(0))
                nc.scalar.copy(xnt[:, :, j * P:(j + 1) * P],
                               misc_p[:].rearrange("p (k t) -> p k t", k=KH)).then_inc(a_c7, 1)

            def last_tap(ch, e):
                act.wait_ge(t_hid, ch.unit(e + 1))
                if not first(ch):
                    act.wait_ge(v_dtu, ch.at(ET, e + 1 - ET))
                    act.wait_ge(a_skip, ch.at(ET, e + 1 - ET))
                ins = nc.scalar.activation(hs[:, e, :], hid_p[:], ACT.Identity, scale=par[:, e, TAPS - 1:TAPS],
                                           bias=par[:, e, TAPS:TAPS + 1])
                if ch.half == 0:
                    if e == 0:
                        act.wait_ge(v_conv, conv_count(ch, 0, 0))
                    ins = nc.scalar.copy(tail[:, e, :], hid_p[:, CH - TAPS + 1:CH])
                ins.then_inc(a_tap, 1)

            def silu_hidden(ch, e):
                act.wait_ge(v_conv, conv_all(ch, e))
                nc.scalar.activation(hs[:, e, :], hs[:, e, :], ACT.Silu).then_inc(a_hs, 1)

            def silu_gate(ch, e):
                act.wait_ge(t_gp, ch.unit(e + 1))
                if e == 0:
                    act.wait_ge(t_out, ch.at(TT, -TT))
                nc.scalar.activation(gy[:, ch.half, e, :], gate_p[:], ACT.Silu).then_inc(a_gs, 1)

            def dt_bc_copy(ch):
                act.wait_ge(t_wx, ch.at(ET, ET))
                act.wait_ge(t_dts, ch.at(ET, 0))
                nc.scalar.copy(dt_t[:], dtacc_p[:]).then_inc(a_dtbc, 1)
                act.wait_ge(s_bc_out, ch.at(16, 0))
                act.wait_ge(v_r, ch.at(R, -R))
                nc.scalar.copy(bc_t, bcacc_p[0:2 * N, :]).then_inc(a_dtbc, 1)

            def skip_term(ch, e):
                act.wait_ge(v_y, ch.unit(e - 1))
                act.wait_ge(a_hs, ch.unit(e + 1))
                nc.scalar.mul(du[:, e % 2, :], hs[:, e, :], par[:, e, TAPS + 2:TAPS + 3]).then_inc(a_skip, 1)

            def softplus(ch, e):
                b = e % 2
                act.wait_ge(v_clamp, ch.unit(e + 1))
                nc.scalar.activation(dts[:, b, :], dts[:, b, :], ACT.Exp).then_inc(a_sp, 1)
                act.wait_ge(a_sp, ch.at(2 * ET, 2 * e + 1))
                nc.scalar.activation(dts[:, b, :], dts[:, b, :], ACT.Ln, bias=1.0).then_inc(a_sp, 1)

            def decay(ch, e, g):
                if g == 0:
                    act.wait_ge(v_dts, ch.unit(e + 1))
                act.wait_ge(v_scan, ch.at(ET * N, e * N + (g + 1 - RING) * GN))
                for k in range(GN):
                    n = g * GN + k
                    ins = nc.scalar.activation(a_buf[:, g % RING, k, :], dts[:, e % 2, :], ACT.Exp,
                                               scale=a_neg[:, e, n:n + 1])
                ins.then_inc(a_exp, 1)

            def xft_copy(ch, j):
                act.wait_ge(t_xft, ch.tile(j + 1))
                act.wait_ge(s_xft_out, ch.at(16 * TT, 16 * j))
                act.wait_ge(t_gate, ch.tile(j))
                act.wait_ge(v_r, ch.at(R, 0))
                if j == 0:
                    act.wait_ge(s_bc_out, 16 * NCHUNK if last(ch) else ch.at(16, 32))
                nc.scalar.copy(xft[:], misc_p[:]).then_inc(a_c7, 1)

            def gate_exp(ch, j):
                act.wait_ge(t_gate, ch.tile(j + 1))
                nc.scalar.activation(score[:, j, :], misc_p[:, 0:NE], ACT.Exp, scale=-1.0).then_inc(a_c7, 1)

            def slot(now, ready, done):
                if now is None and ready is not None:
                    for j in range(TT):
                        xnt_copy(ready, j)
                    for e in range(ET):
                        last_tap(ready, e)
                        silu_hidden(ready, e)
                        silu_gate(ready, e)
                    nc.scalar.preload_act_table_set(EXP_LN_SET)
                    dt_bc_copy(ready)
                    softplus(ready, 0)
                    skip_term(ready, 0)
                    return
                if now is None:
                    for j in range(TT):
                        xft_copy(done, j)
                        gate_exp(done, j)
                    return
                for e in range(ET):
                    for g in range(NG):
                        if e < ET - 1 and g == 6:
                            softplus(now, e + 1)
                        decay(now, e, g)
                        if done is None and g == 3:
                            zero_slots(e)
                        if g == 7 and e + 1 < ET:
                            skip_term(now, e + 1)
                        if g == 6 and e + 1 == ET and ready is not None:
                            skip_term(ready, 0)
                        if done is not None:
                            if 2 <= e <= TT + 1 and g == 0:
                                xft_copy(done, e - 2)
                            if 2 <= e <= TT + 1 and g == 3:
                                gate_exp(done, e - 2)
                        if done is not None and (ET + e, g) == SILU_GATE[-1]:
                            silu_gate(now, ET - 1)
                            nc.scalar.preload_act_table_set(EXP_LN_SET)
                        if ready is None:
                            continue
                        if e == 0 and 2 <= g < 2 + TT:
                            xnt_copy(ready, g - 2)
                        for q in range(ET):
                            if (e, g) == TAP[q]:
                                last_tap(ready, q)
                        for q in range(ET):
                            if (e, g) == SILU_GATE[q]:
                                silu_gate(ready, q)
                            if (e, g) == SILU[q]:
                                silu_hidden(ready, q)
                        if (e, g) in SILU or (e, g) in SILU_GATE:
                            nc.scalar.preload_act_table_set(EXP_LN_SET)
                        if e == ET - 1 and g == 6:
                            dt_bc_copy(ready)
                        if e == ET - 1 and g == 7:
                            softplus(ready, 0)

            run_slots(act, slot)

        @block.tensor
        def _(pe):
            pe.wait_ge(g_setup, 11)
            transpose = nc.tensor.transpose

            def ln1_transpose(ch, j):
                pe.wait_ge(v_ln1, ch.at(3 * TT, 3 * j + 3))
                pe.wait_ge(a_c7, copies7(ch, j, True))
                for k in range(KH):
                    mm = transpose(misc_p[:, k * P:(k + 1) * P], x_in[:, j % 2, k * P:(k + 1) * P], ident[:])
                mm.then_inc(t_ln1, 1)

            def project(ch, e, half):
                if half == 0:
                    pe.wait_ge(s_w[e % 2], ch.at(16 * ET // 2, 16 * (e // 2 + 1)))
                    if e == 0:
                        pe.wait_ge(a_c7, copies7(ch, TT - 1, True) + 1)
                    pe.wait_ge(a_tap, ch.unit(e))
                    pe.wait_ge(v_conv, conv_all(ch, e - 1) if e else conv_count(ch, 0, 0))
                for k in range(half * KH // 2, (half + 1) * KH // 2):
                    mm = nc.tensor.matmul(hid_p[:], wp[:, e % 2, WIN + k * P:WIN + (k + 1) * P], xnt[:, k, :],
                                          start=(k == 0), stop=(k == KH - 1))
                if half == 1:
                    mm.then_inc(t_hid, 1)

            def project_gate(ch, e, half):
                if half == 0:
                    pe.wait_ge(s_wg[e % 2], ch.at(16 * ET // 2, 16 * (e // 2 + 1)))
                    pe.wait_ge(a_gs, ch.unit(e))
                    if e == 0:
                        pe.wait_ge(v_c, ch.at(7 * TT, 7 * (TT - 1) + 3 - 14 * TT))
                for k in range(half * KH // 2, (half + 1) * KH // 2):
                    mm = nc.tensor.matmul(gate_p[:], wg[:, e % 2, k * P:(k + 1) * P],
                                          xnt[:, k, :], start=(k == 0), stop=(k == KH - 1))
                if half == 1:
                    mm.then_inc(t_gp, 1)

            def project_x(ch, e):
                pe.wait_ge(a_hs, ch.unit(e + 1))
                if e == 0:
                    pe.wait_ge(a_dtbc, ch.at(2, 0))
                nc.tensor.matmul(dtacc_p[:], wp[:, e % 2, WX:WX + TR], hs[:, e, :],
                                 start=(e == 0), stop=(e == ET - 1))
                nc.tensor.matmul(bcacc_p[0:2 * N, :], wp[:, e % 2, WX + TR:WX + TR + 2 * N], hs[:, e, :],
                                 start=(e == 0), stop=(e == ET - 1)).then_inc(t_wx, 1)

            def project_dt(ch, e):
                if e == 0:
                    pe.wait_ge(a_dtbc, ch.at(2, 1))
                pe.wait_ge(v_dts, ch.unit(e))
                nc.tensor.matmul(dts_p[:], wdt_sb[:, e, :], dt_t[:],
                                 start=True, stop=True).then_inc(t_dts, 1)

            def sum_states(ch, e, g):
                if g == 0:
                    pe.wait_ge(v_sum_y, ch.unit(e - 1))
                wait_c_product(pe, ch, e, g)
                for k in range(GN):
                    mm = nc.tensor.matmul(y_p[e % 2][:], ident[:], h_buf[:, g % RING, k, :], start=(g == 0 and k == 0),
                                          stop=(g == NG - 1 and k == GN - 1))
                mm.then_inc(t_sum, 1)

            def project_out(ch, j, part):
                if part == 0:
                    pe.wait_ge(v_y, ch.unit(ET))
                    if j == 0:
                        pe.wait_ge(a_gs, last_gate(ch))
                    elif not last(ch):
                        pe.wait_ge(v_c, ch.at(7 * TT, 7 * (j - 1) + 3))
                for k in range(part * ET // 4, (part + 1) * ET // 4):
                    mm = nc.tensor.matmul(out_bank(ch, j)[:], gy[:, ch.half, k, j * P:(j + 1) * P], wout_sb[:, k, :],
                                          start=(k == 0), stop=(k == ET - 1))
                if part == 3:
                    mm.then_inc(t_out, 1)

            def xf_transpose(ch, j):
                pe.wait_ge(v_c, ch.at(7 * TT, 7 * j + 7))
                pe.wait_ge(a_c7, copies7(ch, 2 * j, False))
                for k in range(KH):
                    mm = transpose(misc_p[:, k * P:(k + 1) * P], xf[:, j, k * P:(k + 1) * P], ident[:])
                mm.then_inc(t_xft, 1)

            def gate_logits(ch, j):
                pe.wait_ge(a_c7, copies7(ch, 2 * j, False) + 1)
                for k in range(KH):
                    mm = nc.tensor.matmul(misc_p[:, 0:NE], xft[:, k * P:(k + 1) * P], gate_sb[:, k, :],
                                          start=(k == 0), stop=(k == KH - 1))
                mm.then_inc(t_gate, 1)

            def count_positions(ch):
                pe.wait_ge(v_r, ch.at(R, R_CHOSEN))
                pe.wait_ge(a_c7, copies7(ch, 2 * TT - 1, False) + 1)
                for j in range(TT):
                    for i in range(j + 1):
                        nc.tensor.matmul(misc_p[:, j * NE:(j + 1) * NE], (before if i == j else ones)[:],
                                         chosen[:, i, :], start=(i == 0), stop=(i == j))
                for i in range(TT):
                    mm = nc.tensor.matmul(misc_p[:, TT * NE:(TT + 1) * NE], ones[:], chosen[:, i, :],
                                          start=(i == 0), stop=(i == TT - 1))
                mm.then_inc(t_pos, 1)

            def last_gate(ch):
                return min(ch.unit(2 * ET), NCHUNK * ET) if isinstance(ch.pair, int) else ch.unit(2 * ET)

            def slot(now, ready, done):
                if now is None and ready is not None:
                    for j in range(TT):
                        ln1_transpose(ready, j)
                    for e in range(ET):
                        for half in range(2):
                            project(ready, e, half)
                        if e > 0:
                            project_x(ready, e - 1)
                        for half in range(2):
                            project_gate(ready, e, half)
                    project_x(ready, ET - 1)
                    pe.wait_ge(s_wdt, 16)
                    project_dt(ready, 0)
                    pe.wait_ge(s_const, 48)
                    return
                if now is None:
                    for j in range(TT + 1):
                        if j < TT:
                            for part in range(4):
                                project_out(done, j, part)
                        if j > 0:
                            xf_transpose(done, j - 1)
                            gate_logits(done, j - 1)
                    count_positions(done)
                    return
                for e in range(ET):
                    for g in range(NG):
                        if e < ET - 1 and g == 0:
                            project_dt(now, e + 1)
                        if e == ET - 1 and g == 5 and ready is not None:
                            project_dt(ready, 0)
                        if ready is not None:
                            if e == 0 and 1 <= g <= TT:
                                ln1_transpose(ready, g - 1)
                            for q in range(ET):
                                for half in range(2):
                                    if (e, g) == PROJECT[q][half]:
                                        project(ready, q, half)
                                if (e, g) == TIMES_WX[q]:
                                    project_x(ready, q)
                                for half in range(2):
                                    if (e, g) == GATE[q][half]:
                                        project_gate(ready, q, half)
                        if done is not None:
                            if e < TT and 2 <= g <= 5:
                                project_out(done, e, g - 2)
                            if 1 <= e <= TT and g == 6:
                                xf_transpose(done, e - 1)
                            if 2 <= e <= TT + 1 and g == 1:
                                gate_logits(done, e - 2)
                            if e == 5 and g == 7:
                                count_positions(done)
                        sum_states(now, e, g)

            run_slots(pe, slot)

        @block.vector
        def _(dve):
            V = nc.vector
            V.memset(base[:], 0.0).then_inc(v_setup, 1)
            dve.wait_ge(v_setup, 1)
            dve.wait_ge(g_setup, 11)
            dve.wait_ge(s_par, 16)

            def prepare_stats(ch, j):
                dve.wait_ge(s_x[j % 2], ch.at(8 * TT, 16 * (j // 2 + 1)))
                V.bn_stats(st[:, 0, :], x_in[:, j % 2, :]).then_inc(v_ln1, 1)
                dve.wait_ge(v_ln1, ch.at(3 * TT, 3 * j + 1))
                dve.wait_ge(g_ln1, ch.at(2 * TT, 2 * j))
                apart(dve)
                V.bn_aggr(mv[:, 0, :], st[:, 0, :]).then_inc(v_ln1, 1)

            def prepare_norm(ch, j):
                dve.wait_ge(g_ln1, ch.at(2 * TT, 2 * j + 2))
                V.tensor_scalar(x_in[:, j % 2, :], x_in[:, j % 2, :], mv[:, 0, 0:1], rstd[:, 0:1],
                                ALU.subtract, ALU.mult).then_inc(v_ln1, 1)

            def convolve(ch, e):
                dve.wait_ge(a_tap, ch.unit(e + 1))
                n = 0
                for s in range(1, TAPS):
                    tap = par[:, e, TAPS - 1 - s:TAPS - s]
                    if n:
                        dve.wait_ge(v_conv, conv_count(ch, e, n))
                    V.scalar_tensor_tensor(hs[:, e, s:], hid_p[:, 0:CH - s], tap, hs[:, e, s:],
                                           op0=ALU.mult, op1=ALU.add).then_inc(v_conv, 1)
                    n += 1
                    if ch.half:
                        dve.wait_ge(v_conv, conv_count(ch, e, n))
                        V.scalar_tensor_tensor(hs[:, e, 0:s], tail[:, e, TAPS - 1 - s:], tap, hs[:, e, 0:s],
                                               op0=ALU.mult, op1=ALU.add).then_inc(v_conv, 1)
                        n += 1

            def clamp_dt(ch, e):
                b = e % 2
                dve.wait_ge(t_dts, ch.unit(e + 1))
                dve.wait_ge(a_exp, ch.group(e - 1, 0))
                V.tensor_scalar(dts[:, b, :], dts_p[:], par[:, e, TAPS + 1:TAPS + 2], 40.0,
                                ALU.add, ALU.min).then_inc(v_clamp, 1)

            def finish_dt(ch, e):
                b = e % 2
                dve.wait_ge(a_sp, ch.at(2 * ET, 2 * e + 2))
                V.scalar_tensor_tensor(dts[:, b, :], dts_p[:], par[:, e, TAPS + 1:TAPS + 2], dts[:, b, :],
                                       op0=ALU.add, op1=ALU.max).then_inc(v_dts, 1)
                dve.wait_ge(v_dts, ch.unit(e + 1))
                dve.wait_ge(a_hs, ch.unit(e + 1))
                dve.wait_ge(g_dbu, ch.group(e - 1, 0))
                V.tensor_tensor(dtu[:, b, :], dts[:, b, :], hs[:, e, :], ALU.mult).then_inc(v_dtu, 1)

            def scan(ch, e, g):
                dve.wait_ge(g_dbu, ch.group(e, g + 1))
                dve.wait_ge(a_exp, ch.group(e, g + 1))
                if ch.half:
                    wait_kept(dve, ch.prev(), e, g)
                for k in range(GN):
                    n = g * GN + k
                    V.tensor_tensor_scan(h_buf[:, g % RING, k, :], a_buf[:, g % RING, k, :],
                                         h_buf[:, g % RING, k, :],
                                         state[:, e, n:n + 1] if ch.half else 0.0,
                                         ALU.mult, ALU.add).then_inc(v_scan, 1)

            def keep_state(ch, e, g):
                if ch.half == 0:
                    dve.wait_ge(v_scan, ch.at(ET * N, e * N + (g + 1) * GN))
                    V.tensor_copy(state[:, e, g * GN:(g + 1) * GN], h_buf[:, g % RING, :, CH - 1]
                                  ).then_inc(v_keep, 1)

            def c_product(ch, e, g):
                dve.wait_ge(v_scan, ch.at(ET * N, e * N + (g + 1) * GN))
                wait_kept(dve, ch, e, g)
                if e == 0:
                    dve.wait_ge(s_c[g], ch.at(16, 16))
                V.tensor_tensor(h_buf[:, g % RING], h_buf[:, g % RING],
                                c_bc[:, g * GN:(g + 1) * GN, :], ALU.mult).then_inc(v_cp, 1)

            def gate_y(ch, e):
                dve.wait_ge(t_sum, ch.group(e + 1, 0))
                dve.wait_ge(a_skip, ch.unit(e + 1))
                V.tensor_tensor(du[:, e % 2, :], y_p[e % 2][:], du[:, e % 2, :], ALU.add).then_inc(v_sum_y, 1)
                dve.wait_ge(v_sum_y, ch.unit(e + 1))
                dve.wait_ge(a_gs, ch.unit(e + 1))
                V.tensor_tensor(gy[:, ch.half, e, :], du[:, e % 2, :], gy[:, ch.half, e, :],
                                ALU.mult).then_inc(v_y, 1)

            def finish_step(ch, j, n, ins):
                ins.then_inc(v_c, 1)
                dve.wait_ge(v_c, ch.at(7 * TT, 7 * j + n))

            def finish_stats(ch, j):
                dve.wait_ge(t_out, ch.tile(j + 1))
                finish_step(ch, j, 1, V.bn_stats(st[:, 1, :], out_bank(ch, j)[:]))
                dve.wait_ge(g_c, ch.at(4 * TT, 4 * j))
                apart(dve)
                finish_step(ch, j, 2, V.bn_aggr(mv[:, 1, :], st[:, 1, :]))

            def finish_add(ch, j):
                dve.wait_ge(g_c, ch.at(4 * TT, 4 * j + 2))
                if j == 0:
                    dve.wait_ge(s_scat, ch.at(16 * TT * TOPK, 0))
                    dve.wait_ge(s_zero, 16 * ET)
                finish_step(ch, j, 3, V.tensor_scalar(xf[:, j, :], out_bank(ch, j)[:], mv[:, 1, 0:1], rstd[:, 1:2],
                                                      ALU.subtract, ALU.mult))
                dve.wait_ge(s_x1, ch.at(16 * TT, 16 * (j + 1)))
                finish_step(ch, j, 4, V.tensor_tensor(x1[:], x1[:], xf[:, j, :], ALU.add))

            def finish_second(ch, j):
                finish_step(ch, j, 5, V.bn_stats(st[:, 2, :], x1[:]))
                apart(dve)
                finish_step(ch, j, 6, V.bn_aggr(mv[:, 2, :], st[:, 2, :]))

            def finish_norm(ch, j):
                dve.wait_ge(g_c, ch.at(4 * TT, 4 * j + 4))
                V.tensor_scalar(xf[:, j, :], x1[:], mv[:, 2, 0:1], rstd[:, 2:3],
                                ALU.subtract, ALU.mult).then_inc(v_c, 1)

            def route(ch, part):
                made = [R_PART[part]]

                def step(ins, needed=True):
                    made[0] += 1
                    ins.then_inc(v_r, 1)
                    if needed:
                        dve.wait_ge(v_r, ch.at(R, made[0]))

                def over_k(a):
                    return a.unsqueeze(2).to_broadcast((P, TT, TOPK, NE))

                def flat(a):
                    return a.rearrange("p j k e -> p (j k) e")

                if part == 0:
                    dve.wait_ge(a_c7, copies7(ch, 2 * TT - 1, False) + 1)
                    dve.wait_ge(s_xft_out, ch.at(16 * TT, 16 * TT))
                    step(V.tensor_scalar(score[:], score[:], 1.0, None, ALU.add))
                    step(V.reciprocal(score[:], score[:]))
                    step(V.tensor_tensor(biased[:], score[:], bias_sb[:].unsqueeze(1).to_broadcast((P, TT, NE)),
                                         ALU.add))
                    pairs = biased[:].rearrange("p j (q two) -> p (j q) two", two=2)
                    step(V.tensor_tensor(r_a.rearrange("p q two -> p (q two)"), pairs[:, :, 0], pairs[:, :, 1],
                                         ALU.max), False)
                    step(V.tensor_tensor(r_b.rearrange("p q two -> p (q two)"), pairs[:, :, 0], pairs[:, :, 1],
                                         ALU.min))
                    step(V.tensor_tensor(r_c[:, 0, :], r_a[:, :, 0], r_a[:, :, 1], ALU.max), False)
                    step(V.tensor_tensor(r_c[:, 1, :], r_a[:, :, 0], r_a[:, :, 1], ALU.min), False)
                    step(V.tensor_tensor(r_c[:, 2, :], r_b[:, :, 0], r_b[:, :, 1], ALU.max))
                    step(V.tensor_tensor(r_c[:, 1, :], r_c[:, 1, :], r_c[:, 2, :], ALU.max))
                    step(V.tensor_tensor(gsum.rearrange("p j g -> p (j g)"), r_c[:, 0, :], r_c[:, 1, :], ALU.add))
                if part == 1:
                    other = gsum.unsqueeze(2).to_broadcast((P, TT, NGRP, NGRP))
                    this = gsum.unsqueeze(3).to_broadcast((P, TT, NGRP, NGRP))
                    step(V.tensor_tensor(cmp, other, this, ALU.is_gt), False)
                    step(V.tensor_tensor(cmp2, other, this, ALU.is_equal))
                    step(V.tensor_tensor(cmp2, cmp2,
                                         earlier[:].unsqueeze(1).to_broadcast((P, TT, NGRP, NGRP)), ALU.mult))
                    step(V.tensor_tensor(cmp, cmp, cmp2, ALU.add))
                    step(V.tensor_reduce(rank[:], cmp, AX.X, ALU.add))
                    step(V.tensor_scalar(rank[:], rank[:], float(TOPG), None, ALU.is_lt))
                    in_group = biased[:].rearrange("p j (g s) -> p (j g) s", s=GSZ)
                    step(V.tensor_tensor(in_group, in_group,
                                         rank[:].rearrange("p j g -> p (j g)").unsqueeze(2).to_broadcast(
                                             (P, TT * NGRP, GSZ)), ALU.mult))
                if part == 2:
                    apart(dve)
                    for j in range(TT):
                        step(V.max(top_v[:, j, :], biased[:, j, :]), j == TT - 1)
                    apart(dve)
                    for j in range(TT):
                        step(V.max_index(top_i[:, j, :], top_v[:, j, :], biased[:, j, :]), j == TT - 1)
                if part == 3:
                    step(V.tensor_copy(idx_f[:], top_i[:, :, 0:TOPK]))
                    idx = idx_f[:].rearrange("p j k -> p (j k)")
                    step(V.tensor_tensor(flat(one_hot), iota_f[:].unsqueeze(1).to_broadcast((P, TT * TOPK, NE)),
                                         idx.unsqueeze(2).to_broadcast((P, TT * TOPK, NE)), ALU.is_equal))
                    step(V.tensor_reduce(chosen[:], one_hot.rearrange("p j k e -> p j e k"), AX.X, ALU.add))
                if part == 4:
                    step(V.tensor_tensor(picked, one_hot, over_k(score[:]), ALU.mult))
                    step(V.tensor_reduce(wtmp[:], picked, AX.X, ALU.add))
                    step(V.tensor_reduce(wsum[:], wtmp[:], AX.X, ALU.add))
                    step(V.tensor_scalar(wsum[:], wsum[:], 1e-20, None, ALU.add))
                    step(V.reciprocal(wsum[:], wsum[:]))
                    step(V.tensor_tensor(wtmp[:], wtmp[:], wsum[:].unsqueeze(2).to_broadcast((P, TT, TOPK)),
                                         ALU.mult))
                    step(V.tensor_scalar(wtmp[:], wtmp[:], SCALE, None, ALU.mult))
                if part == 5:
                    dve.wait_ge(t_pos, ch.at(1, 1))
                    per_tile = misc_p[:, 0:TT * NE].rearrange("p (j e) -> p j e", e=NE)
                    step(V.tensor_tensor(pos_all[:], per_tile, base[:].unsqueeze(1).to_broadcast((P, TT, NE)), ALU.add))
                    step(V.tensor_tensor(base[:], misc_p[:, TT * NE:(TT + 1) * NE], base[:], ALU.add))
                    step(V.tensor_tensor(picked, one_hot, over_k(pos_all[:]), ALU.mult))
                    step(V.tensor_reduce(pos[:], picked, AX.X, ALU.add))
                    step(V.scalar_tensor_tensor(slot_f[:], idx_f[:], float(CAP), pos[:], op0=ALU.mult, op1=ALU.add))
                if part == 6:
                    step(V.tensor_scalar(valid[:], pos[:], float(CAP), None, ALU.is_lt))
                    step(V.tensor_tensor(keep_w[:, bass.ds(ch.tile(0), TT), :], wtmp[:], valid[:], ALU.mult), False)
                    step(V.tensor_scalar(pos[:], pos[:], float(CAP), FAR, ALU.is_ge, ALU.mult))
                    step(V.tensor_tensor(slot_f[:], slot_f[:], pos[:], ALU.add))
                    step(V.tensor_copy(keep_slot[:, bass.ds(ch.tile(0), TT), :], slot_f[:]), False)
                    step(V.tensor_copy(slot_now[:], slot_f[:]))
                assert made[0] == R_PART[part + 1]

            def slot(now, ready, done):
                if now is None and ready is not None:
                    for j in range(TT):
                        prepare_stats(ready, j)
                        prepare_norm(ready, j)
                    for e in range(ET):
                        convolve(ready, e)
                    clamp_dt(ready, 0)
                    finish_dt(ready, 0)
                    dve.wait_ge(s_const, 48)
                    return
                if now is None:
                    gate_y(done, ET - 1)
                    for j in range(TT):
                        finish_stats(done, j)
                        finish_add(done, j)
                        finish_second(done, j)
                        finish_norm(done, j)
                    for part in range(len(ROUTE)):
                        route(done, part)
                    return
                for e in range(ET):
                    for g in range(NG):
                        scan(now, e, g)
                        keep_state(now, e, g)
                        if g not in POOL_GROUPS[e]:
                            c_product(now, e, g)
                        if g == 2:
                            if e > 0:
                                gate_y(now, e - 1)
                            elif done is not None:
                                gate_y(done, ET - 1)
                        if g == 2 and e < ET - 1:
                            clamp_dt(now, e + 1)
                        if g == 5 and e < ET - 1:
                            finish_dt(now, e + 1)
                        if ready is not None:
                            if e == 0 and 1 <= g <= TT:
                                prepare_norm(ready, g - 1)
                            if e == 0 and g < TT:
                                prepare_stats(ready, g)
                            for q in range(ET):
                                if (e, g) == CONV[q]:
                                    convolve(ready, q)
                            if e == ET - 1 and g == 6:
                                clamp_dt(ready, 0)
                            if e == ET - 1 and g == 7:
                                finish_dt(ready, 0)
                        if done is not None:
                            if e < TT and g == 7:
                                finish_stats(done, e)
                            if 1 <= e <= TT and g == 1:
                                finish_add(done, e - 1)
                            if 1 <= e <= TT and g == 3:
                                finish_second(done, e - 1)
                            if 1 <= e <= TT and g == 5:
                                finish_norm(done, e - 1)
                            for part in range(len(ROUTE)):
                                if (e, g) == ROUTE[part]:
                                    route(done, part)

            run_slots(dve, slot)


def experts(nc, keep_w, keep_slot, ident, minus_half, sup_t, sdown_t, wexp, out,
            xe_d, ye_d, x1_d, xft_d):
    with ExitStack() as ctx:
        def hold(stack, name, shape, dt=F32):
            return stack.enter_context(nc.sbuf_tensor(name, shape, dt))

        sup = hold(ctx, "sup", [P, KH, HS])
        sdown = hold(ctx, "sdown", [P, KHS, H])
        banks = [ctx.enter_context(nc.psum_tensor(f"bank{i}_p", [P, 512], F32)) for i in range(8)]
        s_shared = ctx.enter_context(nc.semaphore("shared_weights_loaded"))
        run_experts(nc, hold, banks, ident, sup, sdown, s_shared, sup_t, sdown_t, wexp, xe_d, ye_d)
        run_shared(nc, hold, banks, keep_w, keep_slot, minus_half, sup, sdown, s_shared, out,
                   ye_d, x1_d, xft_d)


class Expert:
    NW = 4

    def __init__(self, round_, i):
        self.round, self.i = round_, i

    def back(self, n):
        return Expert(self.round, self.i - n)

    def at(self, per, offset=0):
        return count(self.round * (self.NW * per) + (per * self.i + offset))

    def use(self, ring):
        return self.round * (self.NW // ring) + self.i // ring

    def there(self):
        return not isinstance(self.round, int) or 0 <= self.round * self.NW + self.i < NE


def run_experts(nc, hold, banks, ident, sup, sdown, s_shared, sup_t, sdown_t, wexp, xe_d, ye_d):
    NW = Expert.NW
    TS = CAP // P
    with ExitStack() as ctx:
        def sem(name):
            return ctx.enter_context(nc.semaphore(name))

        we = hold(ctx, "we", [P, NW, 2 * KH * HID])
        xe = hold(ctx, "xe", [P, NW, TS, H])
        xet = hold(ctx, "xet", [P, 2, KH, CAP])
        relu = hold(ctx, "relu", [P, 2, KHID * CAP])
        hid = hold(ctx, "hid", [P, 2, KHID, CAP])
        yo = hold(ctx, "yo", [P, 2, TS, H])
        up_w = we[:, :, 0:KH * HID].rearrange("p w (k m) -> p w k m", k=KH)
        down_w = we[:, :, KH * HID:].rearrange("p w (k d) -> p w k d", k=KHID)
        xt_p, up_p, down_p = banks[0:2], banks[2:4], banks[4:6]

        s_we = [sem(f"expert_weights{i}_loaded") for i in range(NW)]
        s_xe = [sem(f"expert_rows{i}_loaded") for i in range(NW)]
        s_ye = [sem(f"expert_out{i}_stored") for i in range(2)]
        t_x = sem("slots_transposed")
        a_x = sem("slots_copied")
        t_up = sem("up_done")
        a_relu = sem("relu_done")
        v_sq = sem("relu_squared")
        t_down = sem("down_done")
        v_y = sem("expert_out_copied")

        def rounds(eng, body, behind):
            for i in range(NW):
                body(Expert(0, i))
            with eng.Fori(1, NE // NW) as r:
                for i in range(NW):
                    body(Expert(r, i))
            for i in range(behind):
                body(Expert(NE // NW, i))

        def expert_rows(dram, x):
            return dram[bass.ds(x.at(CAP), CAP), :].rearrange("(s p) h -> p s h", p=P)

        block = ctx.enter_context(nc.Block())

        @block.sync
        def _(sp):
            def load(x):
                sp.wait_ge(t_down, x.at(TS, TS * (1 - NW)))
                sp.dma_start(xe[:, x.i], expert_rows(xe_d, x)).then_inc(s_xe[x.i], 16)
                sp.dma_start(we[:, x.i, :], wexp[bass.ds(x.at(1), 1), :, :].rearrange("a p c -> (a p) c")
                             ).then_inc(s_we[x.i], 16)

            rounds(sp, load, 0)
            sp.dma_start(sup[:], sup_t).then_inc(s_shared, 16)
            sp.dma_start(sdown[:], sdown_t).then_inc(s_shared, 16)
            sp.wait_ge(s_shared, 32)

        @block.gpsimd
        def _(pool):
            def store(x):
                pool.wait_ge(v_y, x.at(TS, TS))
                nc.gpsimd.dma_start(expert_rows(ye_d, x), yo[:, x.i % 2]).then_inc(s_ye[x.i % 2], 16)

            rounds(pool, store, 0)
            for s in s_ye:
                pool.wait_ge(s, 16 * NE // 2)

        @block.tensor
        def _(pe):
            def transpose_slots(x):
                pe.wait_ge(s_xe[x.i % NW], (x.use(NW) + 1) * 16)
                for s in range(TS):
                    pe.wait_ge(a_x, x.at(TS, s + 1 - TS))
                    for k in range(KH):
                        mm = nc.tensor.transpose(xt_p[s][:, k * P:(k + 1) * P],
                                                 xe[:, x.i % NW, s, k * P:(k + 1) * P], ident[:])
                    mm.then_inc(t_x, 1)

            def up(x):
                pe.wait_ge(a_x, x.at(TS, TS))
                pe.wait_ge(s_we[x.i % NW], (x.use(NW) + 1) * 16)
                pe.wait_ge(v_sq, x.at(1, -1))
                for m in range(KHID):
                    for k in range(KH):
                        mm = nc.tensor.matmul(up_p[x.i % 2][:, m * CAP:(m + 1) * CAP],
                                              up_w[:, x.i % NW, k, m * P:(m + 1) * P], xet[:, x.i % 2, k, :],
                                              start=(k == 0), stop=(k == KH - 1))
                mm.then_inc(t_up, 1)

            def down(x):
                pe.wait_ge(v_sq, x.at(1, 1))
                for s in range(TS):
                    pe.wait_ge(v_y, x.at(TS, s + 1 - TS))
                    for k in range(KHID):
                        mm = nc.tensor.matmul(down_p[s][:], hid[:, x.i % 2, k, s * P:(s + 1) * P],
                                              down_w[:, x.i % NW, k, :], start=(k == 0), stop=(k == KHID - 1))
                    mm.then_inc(t_down, 1)

            def turn(x):
                for stage, n in ((transpose_slots, 0), (up, 1), (down, 2)):
                    if x.back(n).there():
                        stage(x.back(n))

            rounds(pe, turn, 2)

        @block.scalar
        def _(act):
            def copy_slots(x):
                act.wait_ge(t_up, x.at(1, -1))
                for s in range(TS):
                    act.wait_ge(t_x, x.at(TS, s + 1))
                    nc.scalar.copy(xet[:, x.i % 2, :, s * P:(s + 1) * P],
                                   xt_p[s][:].rearrange("p (k t) -> p k t", k=KH)).then_inc(a_x, 1)

            def relus(x):
                act.wait_ge(t_up, x.at(1, 1))
                act.wait_ge(v_sq, x.at(1, -1))
                nc.scalar.activation(relu[:, x.i % 2, :], up_p[x.i % 2][:], ACT.Relu).then_inc(a_relu, 1)

            def turn(x):
                if x.there():
                    copy_slots(x)
                if x.back(1).there():
                    relus(x.back(1))

            rounds(act, turn, 1)

        @block.vector
        def _(dve):
            V = nc.vector

            def square(x):
                dve.wait_ge(a_relu, x.at(1, 1))
                dve.wait_ge(t_down, x.at(TS, -TS))
                V.tensor_tensor(hid[:, x.i % 2].rearrange("p k c -> p (k c)"), up_p[x.i % 2][:],
                                relu[:, x.i % 2, :], ALU.mult).then_inc(v_sq, 1)

            def copy_out(x):
                dve.wait_ge(s_ye[x.i % 2], x.use(2) * 16)
                for s in range(TS):
                    dve.wait_ge(t_down, x.at(TS, s + 1))
                    V.tensor_copy(yo[:, x.i % 2, s, :], down_p[s][:]).then_inc(v_y, 1)

            def turn(x):
                if x.back(1).there():
                    square(x.back(1))
                if x.back(2).there():
                    copy_out(x.back(2))

            rounds(dve, turn, 2)


def run_shared(nc, hold, banks, keep_w, keep_slot, minus_half, sup, sdown, s_shared, out,
               ye_d, x1_d, xft_d):
    with ExitStack() as ctx:
        def sem(name):
            return ctx.enter_context(nc.semaphore(name))

        xfc = hold(ctx, "xfc", [P, 2, TT, KH * P])
        relu = hold(ctx, "relu_s", [P, 2, CH])
        hsh = hold(ctx, "hsh", [P, 2, KHS, CH])
        rows = hold(ctx, "rows", [P, TT, TOPK, H])
        x1t = hold(ctx, "x1t", [P, TT, H])
        acc = hold(ctx, "acc_f", [P, TT, H])
        slots = hold(ctx, "slots", [P, TT, TOPK], I32)
        st = hold(ctx, "st_f", [P, 6])
        mv = hold(ctx, "mv_f", [P, 2, 2])
        rstd = hold(ctx, "rstd_f", [P, 2])
        up_p, down_p = banks[0:4], banks[4:8]

        s_xfc = [sem(f"xfc{i}_loaded") for i in range(2)]
        s_x1 = [sem(f"x1t{j}_loaded") for j in range(TT)]
        s_rows = [sem(f"rows{j}_gathered") for j in range(TT)]
        s_out = [sem(f"out{j}_stored") for j in range(TT)]
        t_up = sem("shared_up")
        a_relu = sem("shared_relu")
        v_sq = sem("shared_squared")
        t_down = sem("shared_down")
        g_slots = sem("slots_copied_f")
        v_sum = sem("sum_steps")
        g_r = sem("final_rstd")
        v_fin = sem("final_steps")

        x1_tiles = x1_d.rearrange("(i p) h -> i p h", p=P)
        out_tiles = out.rearrange("(i p) h -> i p h", p=P)

        def chunks(eng, slot):
            slot(Chunk(0, 0), None)
            with eng.Fori(0, NPAIR - 1) as r:
                for ready in (Chunk(r, 1), Chunk(r + 1, 0)):
                    slot(ready, ready.prev())
            slot(Chunk(NPAIR - 1, 1), Chunk(NPAIR - 1, 0))
            slot(None, Chunk(NPAIR - 1, 1))

        block = ctx.enter_context(nc.Block())

        @block.sync
        def _(sp):
            def load_xfc(ch):
                sp.wait_ge(t_up, ch.at(KHS, -KHS))
                sp.dma_start(xfc[:, ch.half], xft_d[bass.ds(ch.tile(0), TT), :, :].rearrange("i p c -> p i c")
                             ).then_inc(s_xfc[ch.half], 16)

            def load_x1(ch, j):
                sp.wait_ge(v_fin, ch.at(2 * TT, 2 * (j + 1 - TT)))
                sp.dma_start(x1t[:, j], x1_tiles[bass.ds(ch.tile(j), 1), :, :].rearrange("a p h -> (a p) h")
                             ).then_inc(s_x1[j], 16)

            def store(ch, j):
                sp.wait_ge(v_fin, ch.at(2 * TT, 2 * j + 2))
                sp.dma_start(out_tiles[bass.ds(ch.tile(j), 1), :, :].rearrange("a p h -> (a p) h"),
                             acc[:, j]).then_inc(s_out[j], 16)

            def slot(ready, done):
                if done is None:
                    load_xfc(ready)
                if ready is not None and not (isinstance(ready.pair, int) and ready.at(1) == NCHUNK - 1):
                    load_xfc(ready.next())
                for j in range(TT):
                    if done is not None:
                        store(done, j)
                    if ready is not None:
                        load_x1(ready, j)

            chunks(sp, slot)
            for s in s_out:
                sp.wait_ge(s, 16 * NCHUNK)

        @block.gpsimd
        def _(pool):
            def gather(ch, j):
                nc.gpsimd.tensor_copy(slots[:, j, :], keep_slot[:, bass.ds(ch.tile(j), 1), :].rearrange(
                    "p a k -> p (a k)")).then_inc(g_slots, 1)
                pool.wait_ge(g_slots, ch.tile(j + 1))
                pool.wait_ge(v_sum, ch.at(6 * TT, 6 * j + 4))
                apart(pool)
                for k in range(TOPK):
                    nc.gpsimd.indirect_dma_start(
                        rows[:, j, k, :], None, ye_d,
                        bass.IndirectOffsetOnAxis(ap=slots[:, j, k:k + 1].bitcast(U32), axis=0),
                        bounds_check=NE * CAP - 1, oob_is_err=False).then_inc(s_rows[j], 16)

            def final_rstd(ch, j):
                b = j % 2
                pool.wait_ge(v_sum, ch.at(6 * TT, 6 * (j + TT) + 6))
                apart(pool)
                nc.gpsimd.tensor_scalar(rstd[:, b:b + 1], mv[:, b, 1:2], EPS, None, ALU.add).then_inc(g_r, 1)
                pool.wait_ge(g_r, ch.at(2 * TT, 2 * j + 1))
                nc.gpsimd.tensor_tensor(rstd[:, b:b + 1], rstd[:, b:b + 1], minus_half[:], ALU.pow
                                        ).then_inc(g_r, 1)

            def slot(ready, done):
                for j in range(TT):
                    if done is not None:
                        final_rstd(done, j)
                    if ready is not None:
                        gather(ready, j)

            chunks(pool, slot)

        @block.tensor
        def _(pe):
            pe.wait_ge(s_shared, 32)

            def up(ch, m):
                if m == 0:
                    pe.wait_ge(s_xfc[ch.half], ch.pair * 16 + 16)
                pe.wait_ge(v_sq, ch.at(KHS, m - 3))
                for k in range(KH):
                    mm = nc.tensor.matmul(up_p[m % 4][:].rearrange("p (i t) -> p i t", i=TT),
                                          sup[:, k, m * P:(m + 1) * P],
                                          xfc[:, ch.half, :, k * P:(k + 1) * P],
                                          start=(k == 0), stop=(k == KH - 1))
                mm.then_inc(t_up, 1)

            def down(ch, j):
                if j == 0:
                    pe.wait_ge(v_sq, ch.at(KHS, KHS))
                pe.wait_ge(v_sum, ch.at(6 * TT, 6 * j + 1))
                for m in range(KHS):
                    mm = nc.tensor.matmul(down_p[j][:], hsh[:, ch.half, m, j * P:(j + 1) * P], sdown[:, m, :],
                                          start=(m == 0), stop=(m == KHS - 1))
                mm.then_inc(t_down, 1)

            def slot(ready, done):
                for j in range(TT):
                    if ready is not None:
                        up(ready, 2 * j)
                        up(ready, 2 * j + 1)
                    if done is not None:
                        down(done, j)

            chunks(pe, slot)

        @block.scalar
        def _(act):
            def slot(ready, done):
                if ready is not None:
                    for m in range(KHS):
                        act.wait_ge(t_up, ready.at(KHS, m + 1))
                        act.wait_ge(v_sq, ready.at(KHS, m - 1))
                        nc.scalar.activation(relu[:, m % 2, :], up_p[m % 4][:], ACT.Relu).then_inc(a_relu, 1)

            chunks(act, slot)

        @block.vector
        def _(dve):
            V = nc.vector
            V.memset(rows[:], 0.0).then_inc(v_sum, 6 * TT)
            dve.wait_ge(v_sum, 6 * TT)

            def square(ch, m):
                dve.wait_ge(a_relu, ch.at(KHS, m + 1))
                if m == 0:
                    dve.wait_ge(t_down, ch.at(TT, -TT))
                V.tensor_tensor(hsh[:, ch.half, m, :], up_p[m % 4][:], relu[:, m % 2, :], ALU.mult
                                ).then_inc(v_sq, 1)

            def add_up(ch, j):
                made = [0]

                def step(ins):
                    made[0] += 1
                    ins.then_inc(v_sum, 1)
                    dve.wait_ge(v_sum, ch.at(6 * TT, 6 * (j + TT) + made[0]))

                dve.wait_ge(t_down, ch.tile(j + 1))
                dve.wait_ge(s_rows[j], ch.at(16 * TOPK, 16 * TOPK))
                dve.wait_ge(s_out[j], ch.at(16, 0))
                for k in range(TOPK):
                    weight = keep_w[:, bass.ds(ch.tile(j), 1), k:k + 1].rearrange("p a k -> p (a k)")
                    step(V.scalar_tensor_tensor(acc[:, j, :], rows[:, j, k, :], weight,
                                                acc[:, j, :] if k else down_p[j][:], op0=ALU.mult, op1=ALU.add))
                step(V.bn_stats(st[:], acc[:, j, :]))
                apart(dve)
                step(V.bn_aggr(mv[:, j % 2, :], st[:]))

            def finish(ch, j):
                dve.wait_ge(g_r, ch.at(2 * TT, 2 * j + 2))
                V.tensor_scalar(acc[:, j, :], acc[:, j, :], mv[:, j % 2, 0:1], rstd[:, j % 2:j % 2 + 1],
                                ALU.subtract, ALU.mult).then_inc(v_fin, 1)
                dve.wait_ge(v_fin, ch.at(2 * TT, 2 * j + 1))
                dve.wait_ge(s_x1[j], ch.at(16, 16))
                V.tensor_tensor(acc[:, j, :], acc[:, j, :], x1t[:, j, :], ALU.add).then_inc(v_fin, 1)

            def slot(ready, done):
                for j in range(TT):
                    if ready is not None:
                        square(ready, 2 * j)
                        square(ready, 2 * j + 1)
                    if done is not None:
                        add_up(done, j)
                        if j:
                            finish(done, j - 1)
                if done is not None:
                    finish(done, TT - 1)

            chunks(dve, slot)


def kernel(**inputs):
    import numpy as np
    import concourse.bacc as bacc
    from concourse.bass_utils import run_bass_kernel_spmd

    a = {k: np.ascontiguousarray(v) for k, v in inputs.items()}
    w_in = a["L0_attn_W_in"].reshape(KH, P, 2, ET, P)
    w_in = w_in.transpose(3, 1, 2, 0, 4).reshape(ET, P, 2, KH * P)
    w_x = a["L0_attn_W_x"].reshape(ET, P, TR + 2 * N)
    w_dt = a["L0_attn_W_dt"].reshape(TR, ET, P)

    def channels(v, width=1):
        return v.reshape(ET, P, width).transpose(1, 0, 2)

    def rows(w, k):
        return w.reshape(k, P, -1).transpose(1, 0, 2)

    up = a["L0_ffn_up_w"].transpose(0, 2, 1).reshape(NE, KH, P, HID).transpose(0, 2, 1, 3)
    down = a["L0_ffn_down_w"].transpose(0, 2, 1).reshape(NE, KHID, P, H).transpose(0, 2, 1, 3)
    arrays = {
        "x": a["L0_attn_input_states"].reshape(T, H),
        "wpack": np.concatenate([w_in[:, :, 0], w_x], axis=2),
        "wgate": w_in[:, :, 1],
        "params": np.concatenate([
            channels(a["L0_attn_conv_kernel"], TAPS), channels(a["L0_attn_conv_bias"]),
            channels(a["L0_attn_b_dt"]), channels(a["L0_attn_D"]), channels(a["L0_attn_A_log"], N)], axis=2),
        "w_dt": w_dt,
        "w_out": rows(a["L0_attn_W_out"], ET),
        "gate_t": rows(a["L0_ffn_gate_w"].T, KH),
        "bias_bc": np.broadcast_to(a["L0_ffn_bias_corr"][None, :], (P, NE)),
        "sup_t": rows(a["L0_ffn_shared_up_w"].T, KH),
        "sdown_t": rows(a["L0_ffn_shared_down_w"].T, KHS),
        "wexp": np.concatenate([up.reshape(NE, P, -1), down.reshape(NE, P, -1)], axis=2),
    }
    nc = bacc.Bacc("TRN2", target_bir_lowering=False, num_devices=1, dynamic_dma_scratch_size=4096)
    arrays = {f"in_{k}": np.ascontiguousarray(v) for k, v in arrays.items()}
    args = [nc.dram_tensor(k, v.shape, mybir.dt.from_np(v.dtype), kind="ExternalInput").ap()
            for k, v in arrays.items()]
    args.append(nc.dram_tensor("out_dram", (T, H), F32, kind="ExternalOutput").ap())
    for name, shape in (("xe_scratch", (NE * CAP, H)), ("ye_scratch", (NE * CAP, H)),
                        ("x1_scratch", (T, H)), ("xft_scratch", (NTILE, P, KH * P)),
                        ("bc_scratch", (NCHUNK, 2 * N, CH))):
        args.append(nc.dram_tensor(name, shape, F32, kind="Internal").ap())
    sandwich(nc, *args)
    r = run_bass_kernel_spmd(nc, [arrays], core_ids=[0])
    return r.results[0]["out_dram"].reshape(BATCH, SEQ, H)
```
